# Optimizing a Trainium2 kernel written in Bass

```python
import numpy as np
import jax
import jax.numpy as jnp

def _softmax(x, axis=-1):
    return jax.nn.softmax(x, axis=axis)

def _gelu(x):
    return jax.nn.gelu(x, approximate=True)

def _silu(x):
    return jax.nn.silu(x)

def _sigmoid(x):
    return jax.nn.sigmoid(x)

def _layernorm(x, axis=-1, eps=1e-05):
    m = jnp.mean(x, axis=axis, keepdims=True)
    v = jnp.var(x, axis=axis, keepdims=True)
    return (x - m) / jnp.sqrt(v + eps)

def _scatter_add(tgt, idx, src, axis=0):
    return tgt.at[idx].add(src)

def _segment_sum(src, seg, n):
    return jax.ops.segment_sum(src, seg, n)
kernel_name = 'mk_decoder_postln_d1_seqx_r4_25ef60'

def setup_inputs(seed: int=0):
    np.random.seed(seed)
    _w = jnp.asarray

    def _rec_inputs():
        import jax
        import jax.numpy as jnp
        _rk = jax.random.key(seed)
        x = -0.0002928 + 1 * jax.random.normal(jax.random.fold_in(_rk, 1), (32, 256, 256), jnp.float32)
        _lenS = 256 - jax.random.randint(jax.random.fold_in(_rk, 7), (32,), 0, max(1, 256 // 4) + 1, jnp.int32)
        _lenS2 = 256 - jax.random.randint(jax.random.fold_in(_rk, 8), (32,), 0, max(1, 256 // 4) + 1, jnp.int32)
        _ctx_1024P = jax.random.normal(jax.random.fold_in(_rk, 11), (32, 16, 256), jnp.float32)
        _ctx_1024c = jax.random.dirichlet(jax.random.fold_in(_rk, 511), 0.3 * jnp.ones((16,), jnp.float32), (32, 256))
        _ctx_1024t = jnp.einsum('bsk,bkd->bsd', _ctx_1024c, _ctx_1024P)
        _ctx_1024t = _ctx_1024t * jax.lax.rsqrt(jnp.mean(jnp.square(_ctx_1024t)) + 1e-12) * 0.953939
        ctx_1024 = -1.39393e-06 + 0.999914 * (_ctx_1024t + 0.3 * jax.random.normal(jax.random.fold_in(_rk, 611), (32, 256, 256), jnp.float32))
        return (x, ctx_1024)
    x, ctx_1024 = _rec_inputs()

    def _L0_attn_setup():
        import jax, jax.numpy as jnp
        import numpy as np
        CHUNK = 64
        key = jax.random.key(seed)
        ks = jax.random.split(key, 8)
        d_model, d_inner, n_state, dt_rank, k = (256, 512, 16, 64, 3)
        B, L = (2, 256)
        s = 0.02
        return {'x': jax.random.normal(ks[0], (B, L, d_model), jnp.float32), 'W_in': jax.random.normal(ks[1], (2 * d_inner, d_model), jnp.float32) * s, 'b_in': jnp.zeros((2 * d_inner,), jnp.float32), 'conv_w': jax.random.normal(ks[2], (d_inner, 1, k), jnp.float32) * s, 'conv_b': jnp.zeros((d_inner,), jnp.float32), 'W_x': jax.random.normal(ks[3], (dt_rank + 2 * n_state, d_inner), jnp.float32) * s, 'W_dt': jax.random.normal(ks[4], (d_inner, dt_rank), jnp.float32) * s, 'b_dt': jnp.zeros((d_inner,), jnp.float32), 'A_log': jax.random.normal(ks[5], (d_inner, n_state), jnp.float32), 'W_out': jax.random.normal(ks[6], (d_model, d_inner), jnp.float32) * s, 'b_out': jnp.zeros((d_model,), jnp.float32)}
    _L0_attn_all = _L0_attn_setup()
    _L0_attn_in = {k: v for k, v in _L0_attn_all.items() if k in ('W_in', 'b_in', 'conv_w', 'conv_b', 'W_x', 'W_dt', 'b_dt', 'A_log', 'W_out', 'b_out')}
    del _L0_attn_all

    def _L0_xattn_setup():
        import jax, jax.numpy as jnp
        import numpy as np
        D_MODEL = 256
        N_HEADS = 16
        D_K = D_MODEL // N_HEADS
        key = jax.random.key(seed)
        ks = jax.random.split(key, 11)
        B, S = (2, 512)
        scale = 1.0 / np.sqrt(D_MODEL)
        return {'query': jax.random.normal(ks[0], (B, S, D_MODEL), jnp.float32), 'key': jax.random.normal(ks[1], (B, S, D_MODEL), jnp.float32), 'value': jax.random.normal(ks[2], (B, S, D_MODEL), jnp.float32), 'w_q': jax.random.normal(ks[3], (D_MODEL, D_MODEL), jnp.float32) * scale, 'b_q': jnp.zeros((D_MODEL,), jnp.float32), 'w_k': jax.random.normal(ks[4], (D_MODEL, D_MODEL), jnp.float32) * scale, 'b_k': jnp.zeros((D_MODEL,), jnp.float32), 'w_v': jax.random.normal(ks[5], (D_MODEL, D_MODEL), jnp.float32) * scale, 'b_v': jnp.zeros((D_MODEL,), jnp.float32), 'w_o': jax.random.normal(ks[6], (D_MODEL, D_MODEL), jnp.float32) * scale, 'b_o': jnp.zeros((D_MODEL,), jnp.float32)}
    _L0_xattn_all = _L0_xattn_setup()
    _L0_xattn_in = {k: v for k, v in _L0_xattn_all.items() if k in ('w_q', 'b_q', 'w_k', 'b_k', 'w_v', 'b_v', 'w_o', 'b_o')}
    del _L0_xattn_all

    def _L0_ffn_setup():
        import jax, jax.numpy as jnp
        import numpy as np
        D_MODEL = 256
        D_FF = 704
        N_EXPERTS = 8
        key = jax.random.key(seed)
        k_in, k1, k2, k3 = jax.random.split(key, 4)
        scale = 0.02
        inputs = jax.random.normal(k_in, (4, N_EXPERTS * 512, D_MODEL), dtype=jnp.float32)
        w1 = jax.random.normal(k1, (N_EXPERTS, D_MODEL, D_FF), dtype=jnp.float32) * scale
        w3 = jax.random.normal(k3, (N_EXPERTS, D_MODEL, D_FF), dtype=jnp.float32) * scale
        w2 = jax.random.normal(k2, (N_EXPERTS, D_FF, D_MODEL), dtype=jnp.float32) * scale
        return {'inputs': inputs, 'w1': w1, 'w3': w3, 'w2': w2}
    _L0_ffn_all = _L0_ffn_setup()
    _L0_ffn_in = {k: v for k, v in _L0_ffn_all.items() if k in ('w1', 'w3', 'w2')}
    del _L0_ffn_all
    return {'x': x, 'ctx_1024': ctx_1024, 'L0_attn_W_in': _L0_attn_in['W_in'], 'L0_attn_b_in': _L0_attn_in['b_in'], 'L0_attn_conv_w': _L0_attn_in['conv_w'], 'L0_attn_conv_b': _L0_attn_in['conv_b'], 'L0_attn_W_x': _L0_attn_in['W_x'], 'L0_attn_W_dt': _L0_attn_in['W_dt'], 'L0_attn_b_dt': _L0_attn_in['b_dt'], 'L0_attn_A_log': _L0_attn_in['A_log'], 'L0_attn_W_out': _L0_attn_in['W_out'], 'L0_attn_b_out': _L0_attn_in['b_out'], 'L0_xattn_w_q': _L0_xattn_in['w_q'], 'L0_xattn_b_q': _L0_xattn_in['b_q'], 'L0_xattn_w_k': _L0_xattn_in['w_k'], 'L0_xattn_b_k': _L0_xattn_in['b_k'], 'L0_xattn_w_v': _L0_xattn_in['w_v'], 'L0_xattn_b_v': _L0_xattn_in['b_v'], 'L0_xattn_w_o': _L0_xattn_in['w_o'], 'L0_xattn_b_o': _L0_xattn_in['b_o'], 'L0_ffn_w1': _L0_ffn_in['w1'], 'L0_ffn_w3': _L0_ffn_in['w3'], 'L0_ffn_w2': _L0_ffn_in['w2']}

def reference(x, ctx_1024, L0_attn_W_in, L0_attn_b_in, L0_attn_conv_w, L0_attn_conv_b, L0_attn_W_x, L0_attn_W_dt, L0_attn_b_dt, L0_attn_A_log, L0_attn_W_out, L0_attn_b_out, L0_xattn_w_q, L0_xattn_b_q, L0_xattn_w_k, L0_xattn_b_k, L0_xattn_w_v, L0_xattn_b_v, L0_xattn_w_o, L0_xattn_b_o, L0_ffn_w1, L0_ffn_w3, L0_ffn_w2):
    import jax
    import jax.numpy as jnp

    def _L0_attn_ref(x, W_in, b_in, conv_w, conv_b, W_x, W_dt, b_dt, A_log, W_out, b_out):
        import jax, jax.numpy as jnp
        import numpy as np
        CHUNK = 64
        Bsz, L, _ = x.shape
        d_inner, n_state = A_log.shape
        dt_rank = W_dt.shape[1]
        k = conv_w.shape[-1]
        xr = x @ W_in.T + b_in
        xc, res = jnp.split(xr, 2, axis=-1)
        h = jnp.transpose(xc, (0, 2, 1))
        h = jax.lax.conv_general_dilated(h, conv_w, window_strides=(1,), padding=[(k - 1, 0)], dimension_numbers=('NCH', 'OIH', 'NCH'), feature_group_count=d_inner)
        h = h + conv_b[None, :, None]
        u = jax.nn.silu(jnp.transpose(h, (0, 2, 1)))
        xp = u @ W_x.T
        dlt, Bm, Cm = jnp.split(xp, [dt_rank, dt_rank + n_state], axis=-1)
        delta = jax.nn.softplus(dlt @ W_dt.T + b_dt)
        A = -jnp.exp(A_log)
        dA = jnp.exp(jnp.einsum('bld,dn->bldn', delta, A))
        dBu = jnp.einsum('bld,bln,bld->bldn', delta, Bm, u)
        nc = L // CHUNK
        dA_c = dA.reshape(Bsz, nc, CHUNK, d_inner, n_state).transpose(2, 0, 1, 3, 4)
        dBu_c = dBu.reshape(Bsz, nc, CHUNK, d_inner, n_state).transpose(2, 0, 1, 3, 4)
        C_c = Cm.reshape(Bsz, nc, CHUNK, n_state).transpose(2, 0, 1, 3)

        def step(carry, inp):
            a, bu, c = inp
            carry = a * carry + bu
            y = jnp.einsum('bkdn,bkn->bkd', carry, c)
            return (carry, y)
        init = jnp.zeros((Bsz, nc, d_inner, n_state), x.dtype)
        _, ys = jax.lax.scan(step, init, (dA_c, dBu_c, C_c))
        y = ys.transpose(1, 2, 0, 3).reshape(Bsz, L, d_inner)
        y = y * jax.nn.silu(res)
        return y @ W_out.T + b_out

    def _L0_xattn_ref(query, key, value, w_q, b_q, w_k, b_k, w_v, b_v, w_o, b_o):
        import jax, jax.numpy as jnp
        import numpy as np
        D_MODEL = 256
        N_HEADS = 16
        D_K = D_MODEL // N_HEADS
        B, S, _ = query.shape

        def proj(x, w, b):
            y = jnp.einsum('bsd,ed->bse', x, w) + b
            return y.reshape(B, -1, N_HEADS, D_K).transpose(0, 2, 1, 3)
        q = proj(query, w_q, b_q)
        k = proj(key, w_k, b_k)
        v = proj(value, w_v, b_v)
        scores = jnp.einsum('bhqd,bhkd->bhqk', q, k) / np.sqrt(D_K)
        attn = jax.nn.softmax(scores, axis=-1)
        out = jnp.einsum('bhqk,bhkd->bhqd', attn, v)
        out = out.transpose(0, 2, 1, 3).reshape(B, S, D_MODEL)
        out = jnp.einsum('bsd,ed->bse', out, w_o) + b_o
        return out

    def _L0_ffn_ref(inputs, w1, w3, w2):
        import jax, jax.numpy as jnp
        import numpy as np
        D_MODEL = 256
        D_FF = 704
        N_EXPERTS = 8
        B, T, D = inputs.shape
        E = w1.shape[0]
        C = T // E
        x = inputs.reshape(B, E, C, D)
        gate = jnp.einsum('becd,edf->becf', x, w1)
        up = jnp.einsum('becd,edf->becf', x, w3)
        h = jax.nn.silu(gate) * up
        out = jnp.einsum('becf,efd->becd', h, w2)
        return out.reshape(B, T, D)
    x = _layernorm(x + _L0_attn_ref(x, L0_attn_W_in, L0_attn_b_in, L0_attn_conv_w, L0_attn_conv_b, L0_attn_W_x, L0_attn_W_dt, L0_attn_b_dt, L0_attn_A_log, L0_attn_W_out, L0_attn_b_out), axis=-1)
    x = _layernorm(x + _L0_xattn_ref(x, ctx_1024, ctx_1024, L0_xattn_w_q, L0_xattn_b_q, L0_xattn_w_k, L0_xattn_b_k, L0_xattn_w_v, L0_xattn_b_v, L0_xattn_w_o, L0_xattn_b_o), axis=-1)
    x = _layernorm(x + _L0_ffn_ref(x, L0_ffn_w1, L0_ffn_w3, L0_ffn_w2), axis=-1)
    return x

_drawn_inputs = setup_inputs


def setup_inputs(seed=0):
    import zlib

    import numpy as np

    out = dict(_drawn_inputs(seed))
    spreads = {'L0_attn_b_in': (0.0, 0.8),
     'L0_attn_conv_b': (0.0, 0.8),
     'L0_attn_b_dt': (0.0, 0.8),
     'L0_attn_b_out': (0.0, 0.1),
     'L0_xattn_b_q': (0.0, 0.405),
     'L0_xattn_b_k': (0.0, 0.8),
     'L0_xattn_b_v': (0.0, 0.1),
     'L0_xattn_b_o': (0.0, 0.1)}
    factors = {'L0_attn_W_in': 8.0,
     'L0_attn_conv_w': 8.0,
     'L0_attn_W_x': 8.0,
     'L0_attn_W_dt': 8.0,
     'L0_attn_A_log': 8.0,
     'L0_attn_W_out': 8.0}
    for name, (base, spread) in spreads.items():
        noise = np.random.default_rng([zlib.crc32(name.encode()), seed]).standard_normal(out[name].shape)
        drawn = base * np.exp(spread * noise) if base else spread * noise
        out[name] = jnp.asarray(drawn.astype(out[name].dtype))
    for name, factor in factors.items():
        out[name] = (out[name] * factor).astype(out[name].dtype)
    return out
```

```python
from contextlib import ExitStack

import numpy as np

import concourse.bass as bass
from concourse import mybir

F32 = mybir.dt.float32
F32R = mybir.dt.float32r
ALU = mybir.AluOpType
ACT = mybir.ActivationFunctionType
AX = mybir.AxisListType

P = 128
B, L, D = 32, 256, 256
DI, NS, RANK, TAPS = 512, 16, 64, 3
CH = 64
NCH = L // CH
ND = DI // P
KD = D // P
TT = L // P
H, DK = 16, 16
HG = 4
NG = H // HG
SK = 96
E, FF = 8, 704
FT = (FF + P - 1) // P
FL = FF - (FT - 1) * P
EC = L // E
ET = B * EC
EJ = ET // P
EPS = 1e-5

POOL_STATES = [n for n in range(NS) if n % 4 != 3]
DVE_STATES = [n for n in range(NS) if n not in POOL_STATES]

SLOTS = 16
O_IN = 3
O_CONV = 5
O_SILU = 8
O_XP = 9
O_DT = 10
O_SP = 12
O_LN = 14
O_W = 15
O_SCAN = 18
O_G = O_SCAN + NS + 3
O_OUT = O_G + 2
O_K = 44
O_N1 = 47
O_V = 48
O_X1T = 48
O_Q = 49
O_LD = 52
O_S = 54
O_MT = 59
O_E = 63
O_X1B = 77
O_ON = 70
O_ONT = 84
O_OF = 85
O_LN2 = 94
O_N2 = 95
STEPS_DEEP = O_N2 // SLOTS
UNROLL = 2


class Batch:

    def __init__(self, j, c):
        self.j, self.c, self.par = j, c, c % 2

    def value(self, per_batch, more):
        v = self.c * per_batch + more
        return v if self.j is None else self.j * (UNROLL * per_batch) + v

    def same_parity(self, per_batch):
        v = (self.c // 2 + 1) * per_batch
        return v if self.j is None else self.j * per_batch + v

    def ahead(self, n):
        return Batch(self.j, self.c + n) if self.j is not None else Batch(None, min(self.c + n, B - 1))

    def back(self, n):
        return Batch(self.j, self.c - n) if self.j is not None or self.c >= n else None


def wait(eng, sem, per_batch, batch, more):
    if batch is not None:
        eng.wait_ge(sem, batch.value(per_batch, more))


def wait_all(eng, counts_in, *waits):
    counts = []
    for i, (sem, per, b, more) in enumerate([w for w in waits if w[2] is not None]):
        count = b.value(per, more)
        if b.j is not None:
            eng.reg_mov(counts_in[i], count)
            count = eng.snap(counts_in[i])
        counts.append((sem, count))
    for sem, count in counts:
        eng.wait_ge(sem, count)


class Bank:

    def __init__(self):
        self.last = None

    def wait_read(self, eng, j):
        if self.last:
            sem, per_batch, v = self.last
            eng.wait_ge(sem, v if j is None else j * (UNROLL * per_batch) + v)

    def read_by(self, sem, per_batch, batch, more):
        self.last = (sem, per_batch, batch.c * per_batch + more)

    def leave_loop(self, iterations):
        sem, per_batch, v = self.last
        self.last = (sem, per_batch, v + UNROLL * per_batch * (iterations - 1))


def run_steps(eng, pieces, count, deep, shared=()):
    by_slot = [[(o // SLOTS, f) for o, f in pieces if o % SLOTS == s] for s in range(SLOTS)]

    def step(j, t):
        for slot in by_slot:
            for steps_back, piece in slot:
                c = t - steps_back
                if j is not None or 0 <= c < count:
                    piece(Batch(j, c))

    loop_from = deep + 2 + (count - deep) % UNROLL
    iterations = (count - loop_from) // UNROLL
    for t in range(loop_from):
        step(None, t)
    with eng.Fori(0, iterations) as j:
        for i in range(UNROLL):
            step(j, loop_from + i)
    for bank in shared:
        bank.leave_loop(iterations)
    for t in range(count, count + deep):
        step(None, t)


def number(eng, b):
    return b.value(1, 0) if b.j is None else eng.snap(b.value(1, 0))


def of_batch(eng, dram, b):
    return dram[bass.ds(number(eng, b), 1)].rearrange("a p k t -> (a p) k t")


def mixers(nc, io, x2_dram, q_dram, k_dram, m_dram):
    with ExitStack() as ctx:
        def sb(name, shape, dt=F32):
            return ctx.enter_context(nc.sbuf_tensor(name, shape, dt))

        def sem(name):
            return ctx.enter_context(nc.semaphore(name))

        w_in = sb("w_in", [P, KD, 2 * DI])
        w_x = sb("w_x", [P, ND, RANK + 2 * NS])
        w_dt = sb("w_dt", [RANK + 2 * NS, DI])
        w_out = sb("w_out", [P, ND, D])
        w_q, w_k, w_v, w_o = (sb(n, [P, KD, D]) for n in ("w_q", "w_k", "w_v", "w_o"))
        b_in = sb("b_in", [P, 2 * ND])
        conv_w = sb("conv_w", [P, ND, TAPS])
        conv_b = sb("conv_b", [P, ND])
        b_dt = sb("b_dt", [P, ND])
        a_neg = sb("a_neg", [P, ND, NS])
        b_q, b_k = sb("b_q", [P, KD]), sb("b_k", [P, KD])
        b_out, b_v, b_o = (sb(n, [P, D]) for n in ("b_out_rows", "b_v_rows", "b_o_rows"))
        ident = sb("ident", [P, P])
        sel = sb("sel", [P, 2 * NS, P], F32R)
        one = sb("one", [P, 1])
        eps = sb("eps", [P, 1])
        xT = sb("xT", [P, KD, L])
        xc = sb("xc", [P, ND, TAPS - 1 + L])
        u = sb("u", [P, ND, L])
        gate = sb("gate", [P, 2, ND, L])
        xp = sb("xp", [RANK + 2 * NS, L])
        bcs = sb("bcs", [P, 2, L], F32R)
        z = sb("z", [P, ND, L])
        e = xc[:, :, TAPS - 1:]
        e1 = sb("e1", [P, ND, L])
        g = e1
        delta = sb("delta", [P, 2, ND, L])
        w = sb("w", [P, 2, ND, L])
        dA = sb("dA", [P, 2, ND, NCH, CH])
        dBu = sb("dBu", [P, 4, ND, L])
        h = sb("h", [P, 4, ND, L])
        bc_sb = sb("bc_sb", [P, 4, 2, L])
        x_tok = sb("x_tok", [P, TT, D])
        r1 = sb("r1", [P, TT, D])
        st = sb("st", [P, 2, TT, 6])
        ln_tmp = sb("ln_tmp", [P, 2, 5, TT])
        rstd = sb("rstd", [P, 2, TT])
        shift = sb("shift", [P, 2, TT])
        x1 = sb("x1", [P, 2, TT, D])
        x1b = sb("x1b", [P, TT, D])
        x1T = sb("x1T", [P, KD, L])
        ctxT = sb("ctxT", [P, KD, L])
        parts = sb("parts", [P, 2, KD, L], F32R)
        v = sb("v", [P, 2, TT, H, 2 * DK])
        q_st = sb("q_st", [SK, H, L], F32R)
        k_st = sb("k_st", [SK, H, L], F32R)
        mx = sb("mx", [P, H, TT])
        m_rows = sb("m_rows", [HG * TT, 2, 2, P], F32R)
        probs = sb("probs", [P, 2, TT, L])
        oT = sb("oT", [P, 2, L])
        rsum = sb("rsum", [P, TT, HG])
        on = sb("on", [P, TT, D])
        onT = x1T
        r2 = sb("r2", [P, TT, D])

        def bank(name, shape):
            return ctx.enter_context(nc.psum_tensor(name, shape, F32))

        y_ps = bank("y_ps", [P, ND, L])
        bc_ps = bank("bc_ps", [P, 2, L])
        a_ps = bank("a_ps", [P, 2, L])
        f_ps = bank("f_ps", [P, 2, L])
        s_ps = bank("s_ps", [P, TT, L])
        st_ps = bank("st_ps", [P, TT, L])
        pv_ps = bank("pv_ps", [P, L])

        s_const = sem("const_loaded")
        s_const_v = sem("const_set_dve")
        s_const_a = sem("const_set_act")
        s_xT, s_ctxT, s_xtok = sem("xT_loaded"), sem("ctxT_loaded"), sem("x_tok_loaded")
        s_in_mm = sem("in_proj_done")
        s_in_ev = sem("in_proj_evacuated")
        s_conv1 = sem("conv_partial")
        s_conv = sem("conv_done")
        s_silu = sem("silu_done")
        s_xp_mm, s_xp = sem("x_proj_done"), sem("x_proj_evacuated")
        s_bcs = sem("bc_split")
        s_dt_mm, s_z = sem("dt_proj_done"), sem("z_ready")
        s_sp = sem("softplus_steps")
        s_spv = sem("softplus_steps_dve")
        s_bc_mm, s_bc_sb = sem("bc_broadcast"), sem("bc_in_sbuf")
        s_dA = sem("dA_ready")
        s_dBu_p, s_dBu_v = sem("dBu_pool"), sem("dBu_dve")
        s_scan = sem("scan_done")
        s_hC_p, s_hC_v = sem("hC_pool"), sem("hC_dve")
        s_sum = sem("state_summed")
        s_g = sem("gated")
        s_xb = sem("x_plus_bias")
        s_out_mm = sem("out_proj_done")
        s_r1, s_st1, s_ln1 = sem("residual1"), sem("stats1"), sem("ln1_steps")
        s_lnA1 = sem("ln1_act")
        s_x1 = sem("x1_ready")
        s_x1T_mm, s_x1T = sem("x1T_transposed"), sem("x1T_ready")
        s_q_mm, s_q_hi, s_q_lo = sem("q_done"), sem("q_high"), sem("q_low")
        s_k_mm, s_k_hi, s_k_lo = sem("k_done"), sem("k_high"), sem("k_low")
        s_v_mm, s_v = sem("v_done"), sem("v_ready")
        s_q_dram, s_k_dram = sem("q_in_dram"), sem("k_in_dram")
        s_stack = [sem(f"stack_loaded_{gr}") for gr in range(NG)]
        s_s_mm, s_max = sem("scores_done"), sem("max_done")
        s_mT_mm, s_m_hi, s_m_lo = sem("max_transposed"), sem("max_high"), sem("max_low")
        s_m_dram, s_m_row = sem("max_in_dram"), sem("max_rows_loaded")
        s_st_mm, s_exp = sem("scoresT_done"), sem("probs_ready")
        s_pv, s_oT = sem("pv_done"), sem("oT_evacuated")
        s_on_mm, s_rsum, s_on = sem("heads_transposed"), sem("rsum_ready"), sem("heads_normalised")
        s_onT_mm, s_onT = sem("onT_transposed"), sem("onT_ready")
        s_of_mm = sem("attn_out_done")
        s_x1b = sem("x1_plus_bias")
        s_r2, s_st2, s_ln2 = sem("residual2"), sem("stats2"), sem("ln2_steps")
        s_lnA2 = sem("ln2_act")
        s_x2 = sem("x2_ready")
        s_shift1, s_shift2 = sem("ln1_shift"), sem("ln2_shift")
        s_x2_st = sem("x2_stored")

        NP_, NV_ = len(POOL_STATES), len(DVE_STATES)
        consts = [
            (w_in, "w_in"), (w_x, "w_x"), (w_dt, "w_dt"), (w_out, "w_out"), (w_q, "w_q"), (w_k, "w_k"),
            (w_v, "w_v"), (w_o, "w_o"), (b_in, "b_in"), (conv_w, "conv_w"), (conv_b, "conv_b"),
            (b_dt, "b_dt"), (a_neg, "a_log"), (b_q, "b_q"), (b_k, "b_k"), (ident, "ident"),
        ]
        N_CONST = len(consts) + 3 + 1
        STACK_DMAS = 9

        def state_done(eng, n, batch, sem_p, sem_v):
            if n in POOL_STATES:
                wait(eng, sem_p, NP_, batch, POOL_STATES.index(n) + 1)
            else:
                wait(eng, sem_v, NV_, batch, DVE_STATES.index(n) + 1)

        def over_channels(row):
            return row.unsqueeze(1).to_broadcast([P, ND, L])

        block = ctx.enter_context(nc.Block())

        @block.sync
        def _(sp):
            counts = [sp.alloc_register(f"count_{i}") for i in range(6)]
            for tile, name in consts:
                sp.dma_start(tile[:], io[name]).then_inc(s_const, 16)
            for tile, name in ((b_out, "b_out"), (b_v, "b_v"), (b_o, "b_o")):
                sp.dma_start(tile[:], io[name].partition_broadcast(P)).then_inc(s_const, 16)
            sp.dma_start(h[:].rearrange("p a d t -> p (a d t)"), io["sel"]).then_inc(s_const, 16)
            sp.wait_ge(s_const_v, 10)

            def load_x(b):
                src = of_batch(sp, io["xT"], b)
                wait_all(sp, counts, (s_in_mm, 2 * ND, b.back(1), 2 * ND))
                sp.dma_start(xT[:], src).then_inc(s_xT, 16)

            def load_x_tok(b):
                src = of_batch(sp, io["x_tok"], b)
                wait_all(sp, counts, (s_r1, 1, b.back(1), 1))
                sp.dma_start(x_tok[:], src).then_inc(s_xtok, 16)

            def load_ctx(b):
                src = of_batch(sp, io["ctxT"], b)
                wait_all(sp, counts, (s_k_mm, KD, b.back(1), KD), (s_v_mm, TT, b.back(1), TT))
                sp.dma_start(ctxT[:], src).then_inc(s_ctxT, 16)

            def store_parts(dram, hi, lo, done):
                def piece(b):
                    wait_all(sp, counts, (hi, KD, b, KD), (lo, KD, b, KD),
                             *[(s, STACK_DMAS * 16, b.back(2), STACK_DMAS * 16) for s in s_stack])
                    dst = dram[b.par].rearrange("c (m p) t -> p c m t", p=P)
                    sp.dma_start(dst, parts[:].bitcast(F32)).then_inc(done, 16)
                return piece

            def load_stack(gr):
                def piece(b):
                    heads = slice(HG * gr, HG * gr + HG)
                    wait_all(sp, counts, (s_q_dram, 16, b, 16), (s_k_dram, 16, b, 16),
                             (s_st_mm, H, b.back(1), HG * gr + HG))
                    for row in range(4):
                        rows = slice(DK * row, DK * row + DK)
                        for stack, dram, part in ((q_st, q_dram, row // 2), (k_st, k_dram, row % 2)):
                            src = dram[b.par, part].rearrange("(h i) t -> i h t", i=DK)[:, heads, :]
                            sp.dma_start(stack[rows, heads, :].bitcast(F32), src).then_inc(s_stack[gr], 16)
                    sp.dma_start(q_st[4 * DK:4 * DK + 2, heads, :].bitcast(F32),
                                 k_st[4 * DK + 2:4 * DK + 4, heads, :].bitcast(F32)).then_inc(s_stack[gr], 16)
                return piece

            def store_x2(b):
                rows = x2_dram.rearrange("(a e n r) d -> n e r a d", a=TT, e=P // EC, r=EC)
                rows = rows[bass.ds(number(sp, b), 1)].rearrange("n e r a d -> (n e) r a d")
                wait_all(sp, counts, (s_x2, TT, b, TT))
                for q in range(P // EC):
                    sp.dma_start(rows[q], r2[EC * q:EC * (q + 1)]).then_inc(s_x2_st, 16)

            run_steps(sp, [
                (0, load_x),
                (34, load_x_tok),
                (38, load_ctx),
                (O_K + 2, store_parts(k_dram, s_k_hi, s_k_lo, s_k_dram)),
                (O_Q + 2, store_parts(q_dram, s_q_hi, s_q_lo, s_q_dram)),
                *[(O_LD + HG * gr, load_stack(gr)) for gr in range(NG)],
                (O_N2, store_x2),
            ], B, STEPS_DEEP)
            sp.wait_ge(s_x2_st, 16 * B * (P // EC))
            sp.wait_ge(s_q_dram, 16 * B)
            sp.wait_ge(s_k_dram, 16 * B)
            sp.wait_ge(s_m_dram, 16 * B * NG)

        @block.gpsimd
        def _(pool):
            pool.wait_ge(s_const, 16 * N_CONST)

            def dBu_piece(n):
                def piece(b):
                    wait(pool, s_spv, 4, b, 4)
                    wait(pool, s_bc_sb, NS, b, n + 1)
                    if n >= 4:
                        wait(pool, s_scan, NS, b, n - 3)
                    else:
                        wait(pool, s_scan, NS, b.back(1), NS + n - 3)
                    pool.tensor_tensor(dBu[:, n % 4], w[:, b.par], over_channels(bc_sb[:, n % 4, 0, :]),
                                       ALU.mult).then_inc(s_dBu_p, 1)
                return piece

            def hC_piece(n):
                def piece(b):
                    wait(pool, s_scan, NS, b, n + 1)
                    pool.tensor_tensor(h[:, n % 4], h[:, n % 4], over_channels(bc_sb[:, n % 4, 1, :]),
                                       ALU.mult).then_inc(s_hC_p, 1)
                return piece

            def x_bias(b):
                wait(pool, s_xtok, 16, b, 16)
                pool.tensor_tensor(x_tok[:], x_tok[:], b_out[:].unsqueeze(1).to_broadcast([P, TT, D]),
                                   ALU.add).then_inc(s_xb, 1)

            def x1_bias(b):
                wait(pool, s_x1, TT, b, TT)
                wait(pool, s_r2, 1, b.back(1), 1)
                pool.tensor_tensor(x1b[:], x1[:, b.par], b_o[:].unsqueeze(1).to_broadcast([P, TT, D]),
                                   ALU.add).then_inc(s_x1b, 1)

            run_steps(pool, [
                *[(O_SCAN + n + 1, hC_piece(n)) for n in POOL_STATES],
                *[(O_SCAN + n - 2, dBu_piece(n)) for n in POOL_STATES],
                (36, x_bias),
                (O_X1B, x1_bias),
            ], B, STEPS_DEEP)

        @block.scalar
        def _(act):
            act.wait_ge(s_const, 16 * N_CONST)
            nc.scalar.activation(a_neg[:], a_neg[:], ACT.Exp).then_inc(s_const_a, 1)
            nc.scalar.activation(sel[:].rearrange("p a m -> p (a m)"), h[:].rearrange("p a d t -> p (a d t)"),
                                 ACT.Copy).then_inc(s_const_a, 1)
            act.wait_ge(s_const_v, 9)

            def in_evac(m):
                def piece(b):
                    wait(act, s_in_mm, 2 * ND, b, m // 2 * 2 + 2)
                    if m < ND:
                        wait(act, s_spv, 4, b.back(1), 3)
                        dst = xc[:, m, TAPS - 1:]
                    else:
                        wait(act, s_g, 1, b.back(2), 1)
                        dst = gate[:, b.par, m - ND]
                    nc.scalar.activation(dst, a_ps[:, m % 2, :], ACT.Identity,
                                         bias=b_in[:, m:m + 1]).then_inc(s_in_ev, 1)
                return piece

            def silu(b):
                wait(act, s_in_ev, 2 * ND, b, 2 * ND)
                nc.scalar.activation(gate[:, b.par], gate[:, b.par], ACT.Silu).then_inc(s_silu, 1)
                wait(act, s_conv, ND, b, ND)
                nc.scalar.activation(u[:], u[:], ACT.Silu).then_inc(s_silu, 1)

            def xp_evac(b):
                wait(act, s_xp_mm, 1, b, 1)
                wait(act, s_bcs, 2, b.back(1), 2)
                wait(act, s_dt_mm, ND, b.back(1), ND)
                nc.scalar.activation(xp[:], a_ps[0:RANK + 2 * NS, 0, :], ACT.Copy).then_inc(s_xp, 1)

            def z_evac(d):
                def piece(b):
                    wait(act, s_dt_mm, ND, b, d // 2 * 2 + 2)
                    wait(act, s_spv, 4, b.back(1), 2)
                    nc.scalar.activation(z[:, d], a_ps[:, d % 2, :], ACT.Identity,
                                         bias=b_dt[:, d:d + 1]).then_inc(s_z, 1)
                return piece

            def softplus_exp(b):
                wait(act, s_z, ND, b, ND)
                wait(act, s_spv, 4, b.back(1), 3)
                nc.scalar.activation(e, z[:], ACT.Abs).then_inc(s_sp, 1)
                wait(act, s_sp, 4, b, 1)
                nc.scalar.activation(e, e, ACT.Exp, scale=-1.0).then_inc(s_sp, 1)
                wait(act, s_sp, 4, b, 2)
                wait(act, s_out_mm, TT, b.back(2), TT)
                nc.scalar.activation(e1[:], e, ACT.Identity, bias=one[:, 0:1]).then_inc(s_sp, 1)

            def softplus_ln(b):
                wait(act, s_spv, 4, b, 1)
                wait(act, s_sp, 4, b, 3)
                nc.scalar.activation(e1[:], e1[:], ACT.Ln).then_inc(s_sp, 1)

            def norm_ln(i, s_steps, s_act, s_x):
                def piece(b):
                    wait(act, s_steps, 5, b, 5)
                    wait(act, s_x, TT, b.back(1), TT)
                    nc.scalar.activation(rstd[:, i], ln_tmp[:, i, 4], ACT.Ln, bias=eps[:, 0:1],
                                         scale=1.0 / D).then_inc(s_act, 1)
                return piece

            def norm_exp(i, s_act):
                def piece(b):
                    wait(act, s_act, 2, b, 1)
                    nc.scalar.activation(rstd[:, i], rstd[:, i], ACT.Exp, scale=-0.5).then_inc(s_act, 1)
                return piece

            def decay(n):
                def piece(b):
                    wait(act, s_spv, 4, b, 3)
                    if n >= 2:
                        wait(act, s_scan, NS, b, n - 1)
                    else:
                        wait(act, s_scan, NS, b.back(1), NS + n - 1)
                    for d in range(ND):
                        last = nc.scalar.activation(
                            dA[:, n % 2, d, :, 1:],
                            delta[:, b.par, d].rearrange("p (c t) -> p c t", t=CH)[:, :, 1:],
                            ACT.Exp, scale=a_neg[:, d, n:n + 1])
                    last.then_inc(s_dA, 1)
                return piece

            def bc_evac(n):
                def piece(b):
                    wait(act, s_bc_mm, NS, b, n + 1)
                    state_done(act, (n - 4) % NS, b if n >= 4 else b.back(1), s_hC_p, s_hC_v)
                    nc.scalar.activation(bc_sb[:, n % 4], bc_ps[:], ACT.Copy).then_inc(s_bc_sb, 1)
                return piece

            def x1T_evac(b):
                wait(act, s_x1T_mm, 1, b, 1)
                wait(act, s_of_mm, TT, b.back(3), TT)
                nc.scalar.activation(x1T[:], a_ps[:], ACT.Copy).then_inc(s_x1T, 1)

            def high(bias, s_mm, s_hi, s_dram, steps_back):
                def piece_for(m):
                    def piece(b):
                        wait(act, s_mm, KD, b, KD)
                        wait(act, s_dram, 16, b.back(steps_back), 16)
                        nc.scalar.activation(parts[:, 0, m], a_ps[:, m, :], ACT.Identity,
                                             bias=bias[:, m:m + 1]).then_inc(s_hi, 1)
                    return piece
                return piece_for

            k_high = high(b_k, s_k_mm, s_k_hi, s_q_dram, 1)
            q_high = high(b_q, s_q_mm, s_q_hi, s_k_dram, 0)

            def softmax_exp(hd):
                def piece(b):
                    wait(act, s_st_mm, H, b, hd + 1)
                    if hd >= 2:
                        wait(act, s_pv, H, b, hd - 1)
                    else:
                        wait(act, s_pv, H, b.back(1), H + hd - 1)
                    nc.scalar.activation(probs[:, hd % 2], st_ps[:], ACT.Exp,
                                         scale=float(DK) ** -0.5).then_inc(s_exp, 1)
                return piece

            def oT_evac(gr):
                def piece(b):
                    wait(act, s_pv, H, b, HG * gr + HG)
                    wait(act, s_on_mm, NG, b if gr >= 2 else b.back(1), gr - 1 if gr >= 2 else NG + gr - 1)
                    nc.scalar.activation(oT[:, gr % 2], pv_ps[:], ACT.Copy).then_inc(s_oT, 1)
                return piece

            def onT_evac(b):
                wait(act, s_onT_mm, 1, b, 1)
                wait(act, s_q_mm, KD, b.ahead(2), KD)
                nc.scalar.activation(onT[:], f_ps[:], ACT.Copy).then_inc(s_onT, 1)

            def max_store(gr):
                def piece(b):
                    wait(act, s_m_lo, NG, b, gr + 1)
                    wait(act, s_m_row, NG * 16, b.back(1), 16 * gr + 16)
                    act.dma_start(m_dram[gr].rearrange("c (r t) -> r c t", t=P),
                                  m_rows[:, gr % 2].bitcast(F32)).then_inc(s_m_dram, 16)
                return piece

            def max_load(gr):
                def piece(b):
                    wait(act, s_m_dram, NG * 16, b, 16 * gr + 16)
                    wait(act, s_s_mm, H, b, HG * gr + HG)
                    dst = q_st[4 * DK:4 * DK + 2, HG * gr:HG * gr + HG, :].rearrange("p h t -> p (h t)")
                    act.dma_start(dst.bitcast(F32), m_dram[gr]).then_inc(s_m_row, 16)
                return piece

            run_steps(act, [
                *[(O_MT + HG * gr + 1, max_store(gr)) for gr in range(NG)],
                *[(O_MT + HG * gr + 2, max_load(gr)) for gr in range(NG)],
                *[(O_K + 1, k_high(m)) for m in range(KD)],
                *[(O_Q + 1, q_high(m)) for m in range(KD)],
                *[(O_SCAN + n - 2, bc_evac(n)) for n in range(NS)],
                *[(O_E + HG * gr + HG + 1, oT_evac(gr)) for gr in range(NG)],
                *[(O_E + hd, softmax_exp(hd)) for hd in range(H)],
                *[(O_SCAN + n - 1, decay(n)) for n in range(NS)],
                *[(O_IN + m // 2, in_evac(m)) for m in range(2 * ND)],
                (O_SILU, silu),
                (O_XP, xp_evac),
                *[(O_DT + d // 2, z_evac(d)) for d in range(ND)],
                (O_SP, softplus_exp),
                (O_LN, softplus_ln),
                (O_LN + 32, norm_ln(0, s_ln1, s_lnA1, s_x1)),
                (O_LN2, norm_ln(1, s_ln2, s_lnA2, s_x2)),
                (O_LN + 32, norm_exp(0, s_lnA1)),
                (O_LN2, norm_exp(1, s_lnA2)),
                (O_X1T, x1T_evac),
                (O_ONT, onT_evac),
            ], B, STEPS_DEEP)

        @block.vector
        def _(dve):
            nc.vector.memset(one[:], 1.0).then_inc(s_const_v, 1)
            nc.vector.memset(eps[:], EPS).then_inc(s_const_v, 1)
            nc.vector.memset(xc[:, :, 0:TAPS - 1], 0.0).then_inc(s_const_v, 1)
            nc.vector.memset(dA[:], 0.0).then_inc(s_const_v, 1)
            nc.vector.memset(bcs[:].bitcast(F32), 0.0).then_inc(s_const_v, 1)
            nc.vector.memset(v[:], 1.0).then_inc(s_const_v, 1)
            nc.vector.memset(k_st[4 * DK:SK].bitcast(F32), 0.0).then_inc(s_const_v, 1)
            nc.vector.memset(q_st[4 * DK:SK].bitcast(F32), 0.0).then_inc(s_const_v, 1)
            dve.wait_ge(s_const_a, 1)
            nc.vector.tensor_scalar(a_neg[:], a_neg[:], -1.0, None, ALU.mult).then_inc(s_const_v, 1)
            dve.wait_ge(s_const_v, 7)
            nc.vector.memset(k_st[4 * DK:4 * DK + 2].bitcast(F32), 1.0).then_inc(s_const_v, 1)
            dve.wait_ge(s_const_a, 2)
            dve.wait_ge(s_const, 16 * N_CONST)

            def conv(d):
                def piece(b):
                    wait(dve, s_in_ev, 2 * ND, b, d + 1)
                    wait(dve, s_spv, 4, b.back(1), 4)
                    wait(dve, s_xp_mm, 1, b.back(1), 1)
                    nc.vector.tensor_scalar(u[:, d], xc[:, d, 0:L], conv_w[:, d, 0:1], conv_b[:, d:d + 1],
                                            ALU.mult, ALU.add).then_inc(s_conv1, 1)
                    wait(dve, s_conv1, 2 * ND, b, 2 * d + 1)
                    nc.vector.scalar_tensor_tensor(out=u[:, d], in0=xc[:, d, 1:L + 1], scalar=conv_w[:, d, 1:2],
                                                   in1=u[:, d], op0=ALU.mult, op1=ALU.add).then_inc(s_conv1, 1)
                    wait(dve, s_conv1, 2 * ND, b, 2 * d + 2)
                    nc.vector.scalar_tensor_tensor(out=u[:, d], in0=xc[:, d, 2:L + 2], scalar=conv_w[:, d, 2:3],
                                                   in1=u[:, d], op0=ALU.mult, op1=ALU.add).then_inc(s_conv, 1)
                return piece

            def bc_split(b):
                wait(dve, s_xp, 1, b, 1)
                wait(dve, s_bc_mm, NS, b.back(2), NS)
                bc = xp[RANK:RANK + 2 * NS]
                nc.vector.tensor_copy(bcs[0:2 * NS, b.par], bc).then_inc(s_bcs, 1)
                wait(dve, s_bcs, 2, b, 1)
                nc.vector.tensor_tensor(bcs[2 * NS:4 * NS, b.par], bc, bcs[0:2 * NS, b.par].bitcast(F32),
                                        ALU.subtract).then_inc(s_bcs, 1)

            def softplus_rounding(b):
                wait(dve, s_sp, 4, b, 3)
                nc.vector.scalar_tensor_tensor(out=e, in0=e1[:], scalar=-1.0, in1=e,
                                               op0=ALU.add, op1=ALU.subtract).then_inc(s_spv, 1)
                wait(dve, s_spv, 4, b, 1)
                nc.vector.scalar_tensor_tensor(out=e, in0=z[:], scalar=0.0, in1=e,
                                               op0=ALU.max, op1=ALU.subtract).then_inc(s_spv, 1)

            def softplus_sum(b):
                wait(dve, s_sp, 4, b, 4)
                wait(dve, s_spv, 4, b, 2)
                wait(dve, s_dA, NS, b.back(2), NS)
                nc.vector.tensor_tensor(delta[:, b.par], e, e1[:], ALU.add).then_inc(s_spv, 1)
                wait(dve, s_spv, 4, b, 3)
                wait(dve, s_silu, 2, b, 2)
                nc.vector.tensor_tensor(w[:, b.par], delta[:, b.par], u[:], ALU.mult).then_inc(s_spv, 1)

            def dBu_piece(n):
                def piece(b):
                    wait(dve, s_bc_sb, NS, b, n + 1)
                    wait(dve, s_spv, 4, b, 4)
                    nc.vector.tensor_tensor(dBu[:, n % 4], w[:, b.par], over_channels(bc_sb[:, n % 4, 0, :]),
                                            ALU.mult).then_inc(s_dBu_v, 1)
                return piece

            def scan(n):
                def piece(b):
                    wait(dve, s_dA, NS, b, n + 1)
                    state_done(dve, n, b, s_dBu_p, s_dBu_v)
                    if n >= 4:
                        wait(dve, s_sum, NS, b, n - 3)
                    else:
                        wait(dve, s_sum, NS, b.back(1), NS + n - 3)
                    nc.vector.tensor_tensor_scan(
                        h[:, n % 4].rearrange("p d t -> p (d t)"),
                        dA[:, n % 2].rearrange("p d c t -> p (d c t)"),
                        dBu[:, n % 4].rearrange("p d t -> p (d t)"), 0.0, ALU.mult, ALU.add).then_inc(s_scan, 1)
                return piece

            def hC_piece(n):
                def piece(b):
                    wait(dve, s_scan, NS, b, n + 1)
                    nc.vector.tensor_tensor(h[:, n % 4], h[:, n % 4], over_channels(bc_sb[:, n % 4, 1, :]),
                                            ALU.mult).then_inc(s_hC_v, 1)
                return piece

            def gating(b):
                wait(dve, s_sum, NS, b, NS)
                wait(dve, s_silu, 2, b, 1)
                wait(dve, s_spv, 4, b.ahead(1), 3)
                nc.vector.tensor_tensor(g[:], y_ps[:], gate[:, b.par], ALU.mult).then_inc(s_g, 1)

            def residual(i, r, s_mm, s_add, src_ps, add, s_r, s_st, s_free, free_per):
                def piece(b):
                    wait(dve, s_mm, TT, b, TT)
                    wait(dve, s_add, 1, b, 1)
                    wait(dve, s_free, free_per, b.back(1), free_per)
                    nc.vector.tensor_tensor(r[:], src_ps[:], add[:], ALU.add).then_inc(s_r, 1)
                    wait(dve, s_r, 1, b, 1)
                    for tt in range(TT):
                        nc.vector.bn_stats(st[:, i, tt], r[:, tt]).then_inc(s_st, 1)
                return piece

            def moments(i, s_st, s_steps, s_act):
                def piece(b):
                    wait(dve, s_st, TT, b, TT)
                    wait(dve, s_act, 2, b.back(1), 2)
                    t = ln_tmp[:, i]
                    nc.vector.tensor_tensor(t[:, 0], st[:, i, :, 1], st[:, i, :, 4], ALU.subtract).then_inc(s_steps, 1)
                    nc.vector.tensor_tensor(t[:, 1], st[:, i, :, 2], st[:, i, :, 5], ALU.add).then_inc(s_steps, 1)
                    nc.vector.tensor_tensor(t[:, 2], st[:, i, :, 1], st[:, i, :, 4], ALU.add).then_inc(s_steps, 1)
                    wait(dve, s_steps, 5, b, 1)
                    nc.vector.scalar_tensor_tensor(out=t[:, 3], in0=t[:, 0], scalar=float(D) / 4, in1=t[:, 0],
                                                   op0=ALU.mult, op1=ALU.mult).then_inc(s_steps, 1)
                    wait(dve, s_steps, 5, b, 4)
                    nc.vector.tensor_tensor(t[:, 4], t[:, 1], t[:, 3], ALU.add).then_inc(s_steps, 1)
                return piece

            def normalise(i, r, dst, s_act, s_steps, s_shift, s_x, s_free, free_per, free_back):
                def piece(b):
                    wait(dve, s_act, 2, b, 2)
                    wait(dve, s_steps, 5, b, 5)
                    nc.vector.scalar_tensor_tensor(out=shift[:, i], in0=ln_tmp[:, i, 2], scalar=-0.5,
                                                   in1=rstd[:, i], op0=ALU.mult, op1=ALU.mult).then_inc(s_shift, 1)
                    wait(dve, s_shift, 1, b, 1)
                    if s_free is not None:
                        wait(dve, s_free, free_per, b.back(free_back), free_per)
                    for tt in range(TT):
                        nc.vector.tensor_scalar(dst(b)[:, tt], r[:, tt], rstd[:, i, tt:tt + 1],
                                                shift[:, i, tt:tt + 1], ALU.mult, ALU.add).then_inc(s_x, 1)
                return piece

            def low(bias, s_hi, s_lo):
                def piece_for(m):
                    def piece(b):
                        wait(dve, s_hi, KD, b, KD)
                        nc.vector.scalar_tensor_tensor(out=parts[:, 1, m], in0=a_ps[:, m, :],
                                                       scalar=bias[:, m:m + 1], in1=parts[:, 0, m].bitcast(F32),
                                                       op0=ALU.add, op1=ALU.subtract).then_inc(s_lo, 1)
                    return piece
                return piece_for

            k_low, q_low = low(b_k, s_k_hi, s_k_lo), low(b_q, s_q_hi, s_q_lo)

            def v_evac(b):
                wait(dve, s_v_mm, TT, b, TT)
                wait(dve, s_pv, H, b.back(2), H)
                nc.vector.tensor_tensor(v[:, b.par, :, :, 0:DK],
                                        f_ps[:].rearrange("p a (h i) -> p a h i", i=DK),
                                        b_v[:].rearrange("p (h i) -> p h i", i=DK).unsqueeze(1)
                                        .to_broadcast([P, TT, H, DK]), ALU.add).then_inc(s_v, 1)

            def row_max(hd):
                def piece(b):
                    wait(dve, s_s_mm, H, b, hd + 1)
                    wait(dve, s_mT_mm, NG, b.back(1), hd // HG + 1)
                    nc.vector.tensor_reduce(mx[:, hd], s_ps[:], AX.X, ALU.max).then_inc(s_max, 1)
                return piece

            def max_parts(gr):
                def piece(b):
                    wait(dve, s_mT_mm, NG, b, gr + 1)
                    if gr >= 2:
                        wait(dve, s_m_dram, NG * 16, b, 16 * (gr - 1))
                    else:
                        wait(dve, s_m_dram, NG * 16, b.back(1), 16 * (NG + gr - 1))
                    src = s_ps[0:HG * TT, 0, 0:P]
                    nc.vector.tensor_scalar(m_rows[:, gr % 2, 0], src, -1.0, None, ALU.mult).then_inc(s_m_hi, 1)
                    wait(dve, s_m_hi, NG, b, gr + 1)
                    nc.vector.scalar_tensor_tensor(out=m_rows[:, gr % 2, 1], in0=src, scalar=-1.0,
                                                   in1=m_rows[:, gr % 2, 0].bitcast(F32), op0=ALU.mult,
                                                   op1=ALU.subtract).then_inc(s_m_lo, 1)
                return piece

            def head_norm(gr):
                def piece(b):
                    wait(dve, s_on_mm, NG, b, gr + 1)
                    src = f_ps[:, 0, :].rearrange("p (a h i) -> p a h i", a=TT, h=HG)
                    if gr:
                        wait(dve, s_on, NG, b, gr)
                    else:
                        wait(dve, s_on, NG, b.back(1), NG)
                    nc.vector.reciprocal(rsum[:], src[:, :, :, DK]).then_inc(s_rsum, 1)
                    wait(dve, s_rsum, NG, b, gr + 1)
                    wait(dve, s_onT_mm, 1, b.back(1), 1)
                    dst = on[:, :, HG * DK * gr:HG * DK * (gr + 1)].rearrange("p a (h i) -> p a h i", i=DK)
                    nc.vector.tensor_tensor(dst, src[:, :, :, 0:DK],
                                            rsum[:].unsqueeze(3).to_broadcast([P, TT, HG, DK]),
                                            ALU.mult).then_inc(s_on, 1)
                return piece

            run_steps(dve, [
                (O_G, gating),
                *[(O_SCAN + n + 1, hC_piece(n)) for n in DVE_STATES],
                *[(O_S + hd + 1, row_max(hd)) for hd in range(H)],
                *[(O_SCAN + n, scan(n)) for n in range(NS)],
                *[(O_SCAN + n - 1, dBu_piece(n)) for n in DVE_STATES],
                *[(O_MT + HG * gr, max_parts(gr)) for gr in range(NG)],
                *[(O_CONV + d // 2, conv(d)) for d in range(ND)],
                (O_XP + 1, bc_split),
                (O_SP + 1, softplus_rounding),
                (O_W, softplus_sum),
                (O_OUT + 1, residual(0, r1, s_out_mm, s_xb, a_ps, x_tok, s_r1, s_st1, s_x1, TT)),
                (O_OUT + 2, moments(0, s_st1, s_ln1, s_lnA1)),
                (O_N1, normalise(0, r1, lambda b: x1[:, b.par], s_lnA1, s_ln1, s_shift1, s_x1, s_x1b, 1, 2)),
                *[(O_K + 1, k_low(m)) for m in range(KD)],
                *[(O_Q + 1, q_low(m)) for m in range(KD)],
                (O_V + 1, v_evac),
                *[(O_ON + HG * gr + 1, head_norm(gr)) for gr in range(NG)],
                (O_OF + 1, residual(1, r2, s_of_mm, s_x1b, f_ps, x1b, s_r2, s_st2, s_x2_st, 16 * P // EC)),
                (O_OF + 2, moments(1, s_st2, s_ln2, s_lnA2)),
                (O_N2, normalise(1, r2, lambda b: r2[:], s_lnA2, s_ln2, s_shift2, s_x2, None, 0, 0)),
            ], B, STEPS_DEEP)

        @block.tensor
        def _(pe):
            pe.wait_ge(s_const, 16 * N_CONST)
            pe.wait_ge(s_const_a, 2)
            pe.wait_ge(s_const_v, 10)
            bank_a, bank_f, bank_s = Bank(), Bank(), Bank()

            def mm(out, lhsT, rhs, first, last):
                return nc.tensor.matmul(out, lhsT, rhs, start=first, stop=last)

            def in_proj(m):
                def piece(b):
                    wait(pe, s_xT, 16, b, 16)
                    if m % 2 == 0:
                        bank_a.wait_read(pe, b.j)
                    for k in range(KD):
                        i = mm(a_ps[:, m % 2, :], w_in[:, k, m * P:(m + 1) * P], xT[:, k], k == 0, k == KD - 1)
                    i.then_inc(s_in_mm, 1)
                    bank_a.read_by(s_in_ev, 2 * ND, b, m + 1)
                return piece

            def x_proj(b):
                wait(pe, s_silu, 2, b, 2)
                bank_a.wait_read(pe, b.j)
                for k in range(ND):
                    i = mm(a_ps[0:RANK + 2 * NS, 0, :], w_x[:, k], u[:, k], k == 0, k == ND - 1)
                i.then_inc(s_xp_mm, 1)
                bank_a.read_by(s_xp, 1, b, 1)

            def dt_proj(d):
                def piece(b):
                    wait(pe, s_xp, 1, b, 1)
                    if d % 2 == 0:
                        bank_a.wait_read(pe, b.j)
                    mm(a_ps[:, d % 2, :], w_dt[:, d * P:(d + 1) * P], xp[:], True, True).then_inc(s_dt_mm, 1)
                    bank_a.read_by(s_z, ND, b, d + 1)
                return piece

            def broadcast(n):
                def piece(b):
                    wait(pe, s_bcs, 2, b, 2)
                    wait(pe, s_bc_sb, NS, b if n else b.back(1), n or NS)
                    mm(bc_ps[:, 0, :], sel[:, n], bcs[:, b.par], True, True)
                    mm(bc_ps[:, 1, :], sel[:, NS + n], bcs[:, b.par], True, True).then_inc(s_bc_mm, 1)
                return piece

            def state_sum(n):
                def piece(b):
                    state_done(pe, n, b, s_hC_p, s_hC_v)
                    if n == 0:
                        wait(pe, s_g, 1, b.back(1), 1)
                    for c in range(2):
                        i = mm(y_ps[:, 2 * c:2 * c + 2].rearrange("p d t -> p (d t)"), ident[:],
                               h[:, n % 4, 2 * c:2 * c + 2].rearrange("p d t -> p (d t)"), n == 0, n == NS - 1)
                    i.then_inc(s_sum, 1)
                return piece

            def out_proj(tt):
                def piece(b):
                    wait(pe, s_g, 1, b, 1)
                    if tt == 0:
                        bank_a.wait_read(pe, b.j)
                    for k in range(ND):
                        i = mm(a_ps[:, tt, :], g[:, k, tt * P:(tt + 1) * P], w_out[:, k], k == 0, k == ND - 1)
                    i.then_inc(s_out_mm, 1)
                    bank_a.read_by(s_r1, 1, b, 1)
                return piece

            def k_proj(m):
                def piece(b):
                    wait(pe, s_ctxT, 16, b, 16)
                    if m == 0:
                        bank_a.wait_read(pe, b.j)
                    for k in range(KD):
                        i = mm(a_ps[:, m, :], w_k[:, k, m * P:(m + 1) * P], ctxT[:, k], k == 0, k == KD - 1)
                    i.then_inc(s_k_mm, 1)
                    bank_a.read_by(s_k_lo, KD, b, m + 1)
                return piece

            def v_proj(tt):
                def piece(b):
                    wait(pe, s_ctxT, 16, b, 16)
                    if tt == 0:
                        bank_f.wait_read(pe, b.j)
                    for k in range(KD):
                        i = mm(f_ps[:, tt, :], ctxT[:, k, tt * P:(tt + 1) * P], w_v[:, k], k == 0, k == KD - 1)
                    i.then_inc(s_v_mm, 1)
                    bank_f.read_by(s_v, 1, b, 1)
                return piece

            def transpose(src, s_src, per, s_mm, s_read, bank, dst):
                def piece(b):
                    wait(pe, s_src, per, b, per)
                    bank.wait_read(pe, b.j)
                    for k in range(KD):
                        for tt in range(TT):
                            i = nc.tensor.transpose(dst[:, k, tt * P:(tt + 1) * P],
                                                    src(b)[:, tt, k * P:(k + 1) * P], ident[:])
                    i.then_inc(s_mm, 1)
                    bank.read_by(s_read, 1, b, 1)
                return piece

            def q_proj(m):
                def piece(b):
                    wait(pe, s_x1T, 1, b, 1)
                    if m == 0:
                        bank_a.wait_read(pe, b.j)
                    for k in range(KD):
                        i = mm(a_ps[:, m, :], w_q[:, k, m * P:(m + 1) * P], x1T[:, k], k == 0, k == KD - 1)
                    i.then_inc(s_q_mm, 1)
                    bank_a.read_by(s_q_lo, KD, b, m + 1)
                return piece

            def scores(hd):
                def piece(b):
                    wait(pe, s_stack[hd // HG], STACK_DMAS * 16, b, STACK_DMAS * 16)
                    bank_s.wait_read(pe, b.j)
                    for tt in range(TT):
                        i = mm(s_ps[:, tt], q_st[:, hd, tt * P:(tt + 1) * P], k_st[:, hd], True, True)
                    i.then_inc(s_s_mm, 1)
                    bank_s.read_by(s_max, H, b, hd + 1)
                return piece

            def max_transpose(gr):
                def piece(b):
                    wait(pe, s_max, H, b, HG * gr + HG)
                    bank_s.wait_read(pe, b.j)
                    nc.tensor.transpose(s_ps[0:HG * TT, 0, 0:P],
                                        mx[:, HG * gr:HG * gr + HG].rearrange("p h a -> p (h a)"),
                                        ident[:]).then_inc(s_mT_mm, 1)
                    bank_s.read_by(s_m_lo, NG, b, gr + 1)
                return piece

            def scores_T(hd):
                def piece(b):
                    wait(pe, s_m_row, NG * 16, b, 16 * (hd // HG) + 16)
                    wait(pe, s_exp, H, b if hd else b.back(1), hd or H)
                    for kt in range(TT):
                        i = mm(st_ps[:, kt], k_st[:, hd, kt * P:(kt + 1) * P], q_st[:, hd], True, True)
                    i.then_inc(s_st_mm, 1)
                return piece

            def pv(hd):
                def piece(b):
                    wait(pe, s_exp, H, b, hd + 1)
                    wait(pe, s_v, 1, b, 1)
                    if hd % HG == 0:
                        gr = hd // HG
                        wait(pe, s_oT, NG, b if gr else b.back(1), gr or NG)
                    j = hd % HG
                    for kt in range(TT):
                        i = mm(pv_ps[2 * DK * j:2 * DK * (j + 1)], v[:, b.par, kt, hd], probs[:, hd % 2, kt],
                               kt == 0, kt == TT - 1)
                    i.then_inc(s_pv, 1)
                return piece

            def head_transpose(gr):
                def piece(b):
                    wait(pe, s_oT, NG, b, gr + 1)
                    bank_f.wait_read(pe, b.j)
                    for tt in range(TT):
                        i = nc.tensor.transpose(f_ps[:, 0, tt * P:(tt + 1) * P], oT[:, gr % 2, tt * P:(tt + 1) * P],
                                                ident[:])
                    i.then_inc(s_on_mm, 1)
                    bank_f.read_by(s_on, NG, b, gr + 1)
                return piece

            def attn_out(tt):
                def piece(b):
                    wait(pe, s_onT, 1, b, 1)
                    if tt == 0:
                        bank_f.wait_read(pe, b.j)
                    for k in range(KD):
                        i = mm(f_ps[:, tt, :], onT[:, k, tt * P:(tt + 1) * P], w_o[:, k], k == 0, k == KD - 1)
                    i.then_inc(s_of_mm, 1)
                    bank_f.read_by(s_r2, 1, b, 1)
                return piece

            run_steps(pe, [
                *[(O_SCAN + n - 2, broadcast(n)) for n in range(NS)],
                *[(O_E + hd, scores_T(hd)) for hd in range(H)],
                *[(O_E + hd + 1, pv(hd)) for hd in range(H)],
                *[(O_SCAN + n + 3, state_sum(n)) for n in range(1, NS)],
                *[(O_MT + HG * gr, max_transpose(gr)) for gr in range(NG)],
                *[(O_S + hd, scores(hd)) for hd in range(H)],
                *[(O_IN + m // 2, in_proj(m)) for m in range(2 * ND)],
                (O_XP, x_proj),
                *[(O_DT + d // 2, dt_proj(d)) for d in range(ND)],
                *[(O_OUT, out_proj(tt)) for tt in range(TT)],
                *[(O_K, k_proj(m)) for m in range(KD)],
                *[(O_V, v_proj(tt)) for tt in range(TT)],
                (O_X1T, transpose(lambda b: x1[:, b.par], s_x1, TT, s_x1T_mm, s_x1T, bank_a, a_ps)),
                *[(O_Q, q_proj(m)) for m in range(KD)],
                *[(O_ON + HG * gr, head_transpose(gr)) for gr in range(NG)],
                (O_ONT, transpose(lambda b: on[:], s_on, NG, s_onT_mm, s_onT, bank_f, f_ps)),
                *[(O_OF, attn_out(tt)) for tt in range(TT)],
                (O_SCAN + 3, state_sum(0)),
            ], B, STEPS_DEEP, (bank_a, bank_f, bank_s))


def experts(nc, io, x2_dram, out):
    with ExitStack() as ctx:
        def sb(name, shape, dt=F32):
            return ctx.enter_context(nc.sbuf_tensor(name, shape, dt))

        def sem(name):
            return ctx.enter_context(nc.semaphore(name))

        HALF = ET // 2
        ident = sb("ident_ffn", [P, P])
        eps = sb("eps_ffn", [P, 1])
        w1, w3 = sb("w1", [P, 2, KD, FF]), sb("w3", [P, 2, KD, FF])
        w2 = sb("w2", [P, 2, FT, D])
        x2 = sb("x2", [P, 2, EJ, D])
        x2T = sb("x2T", [P, KD, ET])
        hT = sb("hT", [P, FT, ET])
        silu = sb("silu", [P, 2, HALF])
        st = sb("st_ffn", [P, 2, EJ, 6])
        tmp = sb("ln_tmp_ffn", [P, 5, EJ])
        rstd, shift = sb("rstd_ffn", [P, EJ]), sb("shift_ffn", [P, EJ])

        def bank(name):
            return ctx.enter_context(nc.psum_tensor(name, [P, HALF], F32))

        t_ps, g_ps, u_ps, d_ps = ([bank(f"{n}{i}") for i in range(2)] for n in ("t_ps", "g_ps", "u_ps", "d_ps"))

        f_const, f_const_v = sem("ffn_const_loaded"), sem("ffn_const_set")
        f_x, f_w13, f_w2 = ([sem(f"{n}_loaded_{i}") for i in range(2)] for n in ("x2", "w13", "w2"))
        f_t_mm, f_t = sem("x2T_transposed"), sem("x2T_ready")
        f_g_mm, f_u_mm = sem("gate_done"), sem("up_done")
        f_silu, f_h = sem("silu_ready"), sem("h_ready")
        f_d_mm, f_r, f_st = sem("down_done"), sem("residual3"), sem("stats3")
        f_ln, f_act, f_shift, f_n = sem("ln3_steps"), sem("ln3_act"), sem("ln3_shift"), sem("normalised3")
        f_out = sem("out_stored")
        OUTS = P // EC

        block = ctx.enter_context(nc.Block())

        @block.sync
        def _(sp):
            counts = [sp.alloc_register(f"expert_count_{i}") for i in range(4)]
            sp.dma_start(ident[:], io["ident"]).then_inc(f_const, 16)
            sp.wait_ge(f_const_v, 3)

            def load(b):
                e_at = bass.ds(number(sp, b), 1)
                tokens = x2_dram.rearrange("(e j p) d -> e p j d", e=E, p=P)[e_at]
                wait_all(sp, counts, (f_out, 16 * OUTS, b.back(2), 16 * OUTS))
                sp.dma_start(x2[:, b.par], tokens.rearrange("a p j d -> (a p) j d")).then_inc(f_x[b.par], 16)
                wait_all(sp, counts, (f_d_mm, EJ, b.back(2), EJ))
                for tile, name in ((w1, "w1"), (w3, "w3")):
                    src = io[name].rearrange("e (k p) f -> e p k f", p=P)[e_at]
                    sp.dma_start(tile[:, b.par], src.rearrange("a p k f -> (a p) k f")).then_inc(f_w13[b.par], 16)
                full = (FT - 1) * P
                src = io["w2"][e_at, 0:full].rearrange("a (k p) d -> (a p) k d", p=P)
                sp.dma_start(w2[:, b.par, 0:FT - 1], src).then_inc(f_w2[b.par], 16)
                src = io["w2"][e_at, full:FF].rearrange("a p d -> (a p) d")
                sp.dma_start(w2[0:FL, b.par, FT - 1], src).then_inc(f_w2[b.par], 16)

            def store(b):
                rows = out.rearrange("(j q) (e r) d -> e q r j d", q=OUTS, r=EC)
                rows = rows[bass.ds(number(sp, b), 1)].rearrange("a q r j d -> (a q) r j d")
                wait_all(sp, counts, (f_n, EJ, b, EJ))
                for q in range(OUTS):
                    sp.dma_start(rows[q], x2[EC * q:EC * (q + 1), b.par]).then_inc(f_out, 16)

            run_steps(sp, [(SLOTS + 2, store), (0, load)], E, 1)
            sp.wait_ge(f_out, 16 * OUTS * E)

        @block.scalar
        def _(act):
            act.wait_ge(f_const_v, 3)

            def xT_evac(b):
                wait(act, f_u_mm, 2 * FT, b.back(1), 2 * FT)
                for i in range(2 * KD):
                    wait(act, f_t_mm, 2 * KD, b, i + 1)
                    nc.scalar.activation(x2T[:, i // 2, HALF * (i % 2):HALF * (i % 2 + 1)], t_ps[i % 2][:],
                                         ACT.Copy).then_inc(f_t, 1)

            def gates(b):
                for i in range(2 * FT):
                    m = P if i // 2 < FT - 1 else FL
                    wait(act, f_g_mm, 2 * FT, b, i + 1)
                    if i >= 2:
                        wait(act, f_h, 2 * FT, b, i - 1)
                    else:
                        wait(act, f_h, 2 * FT, b.back(1), 2 * FT + i - 1)
                    nc.scalar.activation(silu[0:m, i % 2], g_ps[i % 2][0:m], ACT.Silu).then_inc(f_silu, 1)

            def norm(b):
                wait(act, f_ln, 5, b, 5)
                wait(act, f_n, EJ, b.back(1), EJ)
                nc.scalar.activation(rstd[:], tmp[:, 4], ACT.Ln, bias=eps[:, 0:1], scale=1.0 / D).then_inc(f_act, 1)
                wait(act, f_act, 2, b, 1)
                nc.scalar.activation(rstd[:], rstd[:], ACT.Exp, scale=-0.5).then_inc(f_act, 1)

            run_steps(act, [(0, xT_evac), (1, gates), (SLOTS + 2, norm)], E, 1)

        @block.vector
        def _(dve):
            nc.vector.memset(eps[:], EPS).then_inc(f_const_v, 1)
            nc.vector.memset(w2[FL:P, :, FT - 1], 0.0).then_inc(f_const_v, 1)
            nc.vector.memset(hT[FL:P, FT - 1], 0.0).then_inc(f_const_v, 1)
            dve.wait_ge(f_const_v, 3)

            def products(b):
                wait(dve, f_d_mm, EJ, b.back(1), EJ)
                for i in range(2 * FT):
                    m = P if i // 2 < FT - 1 else FL
                    wait(dve, f_silu, 2 * FT, b, i + 1)
                    wait(dve, f_u_mm, 2 * FT, b, i + 1)
                    nc.vector.tensor_tensor(hT[0:m, i // 2, HALF * (i % 2):HALF * (i % 2 + 1)], silu[0:m, i % 2],
                                            u_ps[i % 2][0:m], ALU.mult).then_inc(f_h, 1)

            def normalise(b):
                wait(dve, f_act, 2, b, 2)
                nc.vector.scalar_tensor_tensor(out=shift[:], in0=tmp[:, 2], scalar=-0.5, in1=rstd[:],
                                               op0=ALU.mult, op1=ALU.mult).then_inc(f_shift, 1)
                wait(dve, f_shift, 1, b, 1)
                for t in range(EJ):
                    nc.vector.tensor_scalar(x2[:, b.par, t], x2[:, b.par, t], rstd[:, t:t + 1], shift[:, t:t + 1],
                                            ALU.mult, ALU.add).then_inc(f_n, 1)

            def residuals(b):
                for t in range(EJ):
                    wait(dve, f_d_mm, EJ, b, t + 1)
                    nc.vector.tensor_tensor(x2[:, b.par, t], d_ps[t % 2][:, 0:D], x2[:, b.par, t],
                                            ALU.add).then_inc(f_r, 1)
                    wait(dve, f_r, EJ, b, t + 1)
                    nc.vector.bn_stats(st[:, b.par, t], x2[:, b.par, t]).then_inc(f_st, 1)

            def moments(b):
                wait(dve, f_st, EJ, b, EJ)
                s = st[:, b.par]
                nc.vector.tensor_tensor(tmp[:, 0], s[:, :, 1], s[:, :, 4], ALU.subtract).then_inc(f_ln, 1)
                nc.vector.tensor_tensor(tmp[:, 1], s[:, :, 2], s[:, :, 5], ALU.add).then_inc(f_ln, 1)
                nc.vector.tensor_tensor(tmp[:, 2], s[:, :, 1], s[:, :, 4], ALU.add).then_inc(f_ln, 1)
                wait(dve, f_ln, 5, b, 1)
                nc.vector.scalar_tensor_tensor(out=tmp[:, 3], in0=tmp[:, 0], scalar=float(D) / 4, in1=tmp[:, 0],
                                               op0=ALU.mult, op1=ALU.mult).then_inc(f_ln, 1)
                wait(dve, f_ln, 5, b, 4)
                nc.vector.tensor_tensor(tmp[:, 4], tmp[:, 1], tmp[:, 3], ALU.add).then_inc(f_ln, 1)

            run_steps(dve, [(1, products), (SLOTS + 2, normalise), (3, residuals), (4, moments)], E, 1)

        @block.tensor
        def _(pe):
            pe.wait_ge(f_const, 16)
            pe.wait_ge(f_const_v, 3)

            def transposes(b):
                pe.wait_ge(f_x[b.par], b.same_parity(16))
                for i in range(2 * KD):
                    if i >= 2:
                        wait(pe, f_t, 2 * KD, b, i - 1)
                    else:
                        wait(pe, f_t, 2 * KD, b.back(1), 2 * KD + i - 1)
                    k = i // 2
                    for t in range(EJ // 2):
                        ins = nc.tensor.transpose(t_ps[i % 2][:, t * P:(t + 1) * P],
                                                  x2[:, b.par, EJ // 2 * (i % 2) + t, k * P:(k + 1) * P], ident[:])
                    ins.then_inc(f_t_mm, 1)

            def gate_up(b):
                wait(pe, f_t, 2 * KD, b, 2 * KD)
                pe.wait_ge(f_w13[b.par], b.same_parity(32))
                for i in range(2 * FT):
                    f0 = P * (i // 2)
                    m = min(P, FF - f0)
                    cols = slice(HALF * (i % 2), HALF * (i % 2 + 1))
                    for w_, ps, done, read in ((w1, g_ps, f_g_mm, f_silu), (w3, u_ps, f_u_mm, f_h)):
                        if i >= 2:
                            wait(pe, read, 2 * FT, b, i - 1)
                        else:
                            wait(pe, read, 2 * FT, b.back(1), 2 * FT + i - 1)
                        for k in range(KD):
                            ins = nc.tensor.matmul(ps[i % 2][0:m], w_[:, b.par, k, f0:f0 + m], x2T[:, k, cols],
                                                   start=(k == 0), stop=(k == KD - 1))
                        ins.then_inc(done, 1)

            def down(b):
                pe.wait_ge(f_w2[b.par], b.same_parity(32))
                wait(pe, f_h, 2 * FT, b, 2 * FT)
                for t in range(EJ):
                    if t >= 2:
                        wait(pe, f_r, EJ, b, t - 1)
                    else:
                        wait(pe, f_r, EJ, b.back(1), EJ + t - 1)
                    for k in range(FT):
                        ins = nc.tensor.matmul(d_ps[t % 2][:, 0:D], hT[:, k, t * P:(t + 1) * P], w2[:, b.par, k],
                                               start=(k == 0), stop=(k == FT - 1))
                    ins.then_inc(f_d_mm, 1)

            run_steps(pe, [(0, transposes), (1, gate_up), (3, down)], E, 1)


def decoder_layer(nc, io, out):
    x2_dram = nc.dram_tensor("x2_rows", (E * ET, D), F32, kind="Internal").ap()
    q_dram = nc.dram_tensor("q_parts_dram", (2, 2, D, L), F32, kind="Internal").ap()
    k_dram = nc.dram_tensor("k_parts_dram", (2, 2, D, L), F32, kind="Internal").ap()
    m_dram = nc.dram_tensor("max_rows_dram", (NG, 2, HG * L), F32, kind="Internal").ap()
    mixers(nc, io, x2_dram, q_dram, k_dram, m_dram)
    experts(nc, io, x2_dram, out)


def layouts(inputs):
    def columns(a, *shape):
        a = np.asarray(a)
        return a.reshape(-1, P, *a.shape[1:]).swapaxes(0, 1).reshape(P, -1, *shape)

    def tokens_last(a):
        return np.asarray(a).transpose(0, 2, 1).reshape(B, KD, P, L).transpose(0, 2, 1, 3)

    i = {k.removeprefix("L0_"): np.asarray(a) for k, a in inputs.items()}
    selector = np.zeros((P, 2 * NS, P), np.float32)
    for n in range(2 * NS):
        selector[[n, 2 * NS + n], n] = 1.0
    return {
        "xT": tokens_last(i["x"]),
        "x_tok": i["x"].reshape(B, TT, P, D).transpose(0, 2, 1, 3),
        "ctxT": tokens_last(i["ctx_1024"]),
        "w_in": columns(i["attn_W_in"].T, 2 * DI),
        "w_x": columns(i["attn_W_x"].T, RANK + 2 * NS),
        "w_dt": np.concatenate([i["attn_W_dt"].T, np.zeros((2 * NS, DI), np.float32)]),
        "w_out": columns(i["attn_W_out"].T, D),
        "w_q": columns(i["xattn_w_q"].T, D), "w_k": columns(i["xattn_w_k"].T, D),
        "w_v": columns(i["xattn_w_v"].T, D), "w_o": columns(i["xattn_w_o"].T, D),
        "b_in": columns(i["attn_b_in"]), "conv_w": columns(i["attn_conv_w"][:, 0], TAPS),
        "conv_b": columns(i["attn_conv_b"]), "b_dt": columns(i["attn_b_dt"]),
        "a_log": columns(i["attn_A_log"], NS),
        "b_q": columns(i["xattn_b_q"]), "b_k": columns(i["xattn_b_k"]),
        "b_out": i["attn_b_out"], "b_v": i["xattn_b_v"], "b_o": i["xattn_b_o"],
        "w1": i["ffn_w1"], "w3": i["ffn_w3"], "w2": i["ffn_w2"],
        "ident": np.eye(P, dtype=np.float32),
        "sel": selector.reshape(P, 2 * NS * P),
    }


def kernel(**inputs):
    import concourse.bacc as bacc
    from concourse.bass_utils import run_bass_kernel_spmd

    nc = bacc.Bacc("TRN2", target_bir_lowering=False, num_devices=1)
    arrays = {f"in_{k}": np.ascontiguousarray(a) for k, a in layouts(inputs).items()}
    io = {k.removeprefix("in_"): nc.dram_tensor(k, a.shape, mybir.dt.from_np(a.dtype), kind="ExternalInput").ap()
          for k, a in arrays.items()}
    out = nc.dram_tensor("out", (B, L, D), F32, kind="ExternalOutput").ap()
    decoder_layer(nc, io, out)
    result = run_bass_kernel_spmd(nc, [arrays], core_ids=[0])
    return result.results[0]["out"]
```

```python
from contextlib import ExitStack

import numpy as np

import concourse.bass as bass
from concourse import mybir

F32 = mybir.dt.float32
F32R = mybir.dt.float32r
ALU = mybir.AluOpType
ACT = mybir.ActivationFunctionType
AX = mybir.AxisListType

P = 128
B, L, D = 32, 256, 256
DI, NS, RANK, TAPS = 512, 16, 64, 3
CH = 64
NCH = L // CH
ND = DI // P
KD = D // P
TT = L // P
H, DK = 16, 16
HG = 4
NG = H // HG
SK = 96
E, FF = 8, 704
FT = (FF + P - 1) // P
FL = FF - (FT - 1) * P
EC = L // E
ET = B * EC
EJ = ET // P
EPS = 1e-5

POOL_STATES = [n for n in range(NS) if n % 4 != 2]
DVE_STATES = [n for n in range(NS) if n not in POOL_STATES]
PAIRED = [3, 7, 11, 15]
SUMMED = [n for n in range(NS) if n + 1 not in PAIRED]

SLOTS = 16
O_IN = 3
O_CONV = 5
O_SILU = 8
O_XP = 9
O_DT = 10
O_SP = 12
O_LN = 14
O_W = 15
O_SCAN = 18
O_G = O_SCAN + NS + 3
O_OUT = O_G + 2
O_K = 44
O_N1 = 47
O_V = 48
O_X1T = 48
O_Q = 49
O_LD = 52
O_S = 54
O_MT = 59
O_E = 63
O_X1B = 77
O_ON = 70
O_ONT = 84
O_OF = 85
O_LN2 = 94
O_N2 = 95
STEPS_DEEP = O_N2 // SLOTS
UNROLL = 2


class Batch:

    def __init__(self, j, c):
        self.j, self.c, self.par = j, c, c % 2

    def value(self, per_batch, more):
        v = self.c * per_batch + more
        return v if self.j is None else self.j * (UNROLL * per_batch) + v

    def same_parity(self, per_batch):
        v = (self.c // 2 + 1) * per_batch
        return v if self.j is None else self.j * per_batch + v

    def ahead(self, n):
        return Batch(self.j, self.c + n) if self.j is not None else Batch(None, min(self.c + n, B - 1))

    def back(self, n):
        return Batch(self.j, self.c - n) if self.j is not None or self.c >= n else None


def wait_all(eng, counts_in, *waits):
    counts = []
    for i, (sem, per, b, more) in enumerate([w for w in waits if w[2] is not None]):
        count = b.value(per, more)
        if b.j is not None:
            eng.reg_mov(counts_in[i], count)
            count = eng.snap(counts_in[i])
        counts.append((sem, count))
    for sem, count in counts:
        eng.wait_ge(sem, count)


class Bank:

    def __init__(self):
        self.last = None

    def wait_read(self, eng, j):
        if self.last:
            sem, per_batch, v = self.last
            eng.wait_ge(sem, v if j is None else j * (UNROLL * per_batch) + v)

    def read_by(self, sem, per_batch, batch, more):
        self.last = (sem, per_batch, batch.c * per_batch + more)

    def leave_loop(self, iterations):
        sem, per_batch, v = self.last
        self.last = (sem, per_batch, v + UNROLL * per_batch * (iterations - 1))


def run_steps(eng, pieces, count, deep, shared=()):
    by_slot = [[(o // SLOTS, f) for o, f in pieces if o % SLOTS == s] for s in range(SLOTS)]

    def step(j, t):
        for slot in by_slot:
            for steps_back, piece in slot:
                c = t - steps_back
                if j is not None or 0 <= c < count:
                    piece(Batch(j, c))

    loop_from = deep + 2 + (count - deep) % UNROLL
    iterations = (count - loop_from) // UNROLL
    for t in range(loop_from):
        step(None, t)
    with eng.Fori(0, iterations) as j:
        for i in range(UNROLL):
            step(j, loop_from + i)
    for bank in shared:
        bank.leave_loop(iterations)
    for t in range(count, count + deep):
        step(None, t)


def number(eng, b):
    return b.value(1, 0) if b.j is None else eng.snap(b.value(1, 0))


def of_batch(eng, dram, b):
    return dram[bass.ds(number(eng, b), 1)].rearrange("a p k t -> (a p) k t")


def mixers(nc, io, x2_dram, q_dram, k_dram, m_dram):
    with ExitStack() as ctx:
        def sb(name, shape, dt=F32):
            return ctx.enter_context(nc.sbuf_tensor(name, shape, dt))

        def sem(name):
            return ctx.enter_context(nc.semaphore(name))

        w_in = sb("w_in", [P, KD, 2 * DI])
        w_x = sb("w_x", [P, ND, RANK + 2 * NS])
        w_dt = sb("w_dt", [RANK + 2 * NS, DI])
        w_out = sb("w_out", [P, ND, D])
        w_q, w_k, w_v, w_o = (sb(n, [P, KD, D]) for n in ("w_q", "w_k", "w_v", "w_o"))
        b_in = sb("b_in", [P, 2 * ND])
        conv_w = sb("conv_w", [P, ND, TAPS])
        conv_b = sb("conv_b", [P, ND])
        b_dt = sb("b_dt", [P, ND])
        a_neg = sb("a_neg", [P, ND, NS])
        b_q, b_k = sb("b_q", [P, KD]), sb("b_k", [P, KD])
        b_out, b_v, b_o = (sb(n, [P, D]) for n in ("b_out_rows", "b_v_rows", "b_o_rows"))
        ident = sb("ident", [P, P])
        sel = sb("sel", [P, 2 * NS, P], F32R)
        one = sb("one", [P, 1])
        eps = sb("eps", [P, 1])
        xT = sb("xT", [P, KD, L])
        xc = sb("xc", [P, ND, TAPS - 1 + L])
        u = sb("u", [P, ND, L])
        gate = sb("gate", [P, 2, ND, L])
        xp = sb("xp", [RANK + 2 * NS, L])
        bcs = sb("bcs", [P, 2, L], F32R)
        z = sb("z", [P, ND, L])
        e = xc[:, :, TAPS - 1:]
        e1 = sb("e1", [P, ND, L])
        g = e1
        delta = sb("delta", [P, 2, ND, L])
        w = sb("w", [P, 2, ND, L])
        dA = sb("dA", [P, 2, ND, NCH, CH])
        dBu = sb("dBu", [P, 4, ND, L])
        h = sb("h", [P, 4, ND, L])
        bc_sb = sb("bc_sb", [P, 4, 2, L])
        x_tok = sb("x_tok", [P, TT, D])
        r1 = sb("r1", [P, TT, D])
        st = sb("st", [P, 2, TT, 6])
        ln_tmp = sb("ln_tmp", [P, 2, 5, TT])
        rstd = sb("rstd", [P, 2, TT])
        shift = sb("shift", [P, 2, TT])
        x1 = sb("x1", [P, 2, TT, D])
        x1b = sb("x1b", [P, TT, D])
        x1T = sb("x1T", [P, KD, L])
        ctxT = sb("ctxT", [P, KD, L])
        parts = sb("parts", [P, 2, KD, L], F32R)
        v = sb("v", [P, 2, TT, H, 2 * DK])
        q_st = sb("q_st", [SK, H, L], F32R)
        k_st = sb("k_st", [SK, H, L], F32R)
        mx = sb("mx", [P, H, TT])
        m_rows = sb("m_rows", [HG * TT, 2, 2, P], F32R)
        probs = sb("probs", [P, 2, TT, L])
        oT = sb("oT", [P, 2, L])
        rsum = sb("rsum", [P, TT, HG])
        on = sb("on", [P, TT, D])
        onT = x1T
        r2 = sb("r2", [P, TT, D])

        def bank(name, shape):
            return ctx.enter_context(nc.psum_tensor(name, shape, F32))

        y_ps = bank("y_ps", [P, ND, L])
        bc_ps = bank("bc_ps", [P, 2, L])
        a_ps = bank("a_ps", [P, 2, L])
        f_ps = bank("f_ps", [P, 2, L])
        s_ps = bank("s_ps", [P, TT, L])
        st_ps = bank("st_ps", [P, TT, L])
        pv_ps = bank("pv_ps", [P, L])

        s_const = sem("const_loaded")
        s_const_v = sem("const_set_dve")
        s_const_a = sem("const_set_act")
        s_xT, s_ctxT, s_xtok = sem("xT_loaded"), sem("ctxT_loaded"), sem("x_tok_loaded")
        s_in_mm = sem("in_proj_done")
        s_in_ev = sem("in_proj_evacuated")
        s_conv1 = sem("conv_partial")
        s_conv = sem("conv_done")
        s_silu = sem("silu_done")
        s_xp_mm, s_xp = sem("x_proj_done"), sem("x_proj_evacuated")
        s_bcs = sem("bc_split")
        s_dt_mm, s_z = sem("dt_proj_done"), sem("z_ready")
        s_sp = sem("softplus_steps")
        s_spv = sem("softplus_steps_dve")
        s_bc_mm, s_bc_sb = sem("bc_broadcast"), sem("bc_in_sbuf")
        s_dA = sem("dA_ready")
        s_dBu_p, s_dBu_v = sem("dBu_pool"), sem("dBu_dve")
        s_scan = sem("scan_done")
        s_hC_p, s_hC_v = sem("hC_pool"), sem("hC_dve")
        s_pair = sem("pair_added")
        s_sum = sem("product_summed")
        s_g = sem("gated")
        s_xb = sem("x_plus_bias")
        s_out_mm = sem("out_proj_done")
        s_r1, s_st1, s_ln1 = sem("residual1"), sem("stats1"), sem("ln1_steps")
        s_lnA1 = sem("ln1_act")
        s_x1 = sem("x1_ready")
        s_x1T_mm, s_x1T = sem("x1T_transposed"), sem("x1T_ready")
        s_q_mm, s_q_hi, s_q_lo = sem("q_done"), sem("q_high"), sem("q_low")
        s_k_mm, s_k_hi, s_k_lo = sem("k_done"), sem("k_high"), sem("k_low")
        s_v_mm, s_v = sem("v_done"), sem("v_ready")
        s_q_dram, s_k_dram = sem("q_in_dram"), sem("k_in_dram")
        s_stack = [sem(f"stack_loaded_{gr}") for gr in range(NG)]
        s_s_mm, s_max = sem("scores_done"), sem("max_done")
        s_mT_mm, s_m_hi, s_m_lo = sem("max_transposed"), sem("max_high"), sem("max_low")
        s_m_dram, s_m_row = sem("max_in_dram"), sem("max_rows_loaded")
        s_st_mm, s_exp = sem("scoresT_done"), sem("probs_ready")
        s_pv, s_oT = sem("pv_done"), sem("oT_evacuated")
        s_on_mm, s_rsum, s_on = sem("heads_transposed"), sem("rsum_ready"), sem("heads_normalised")
        s_onT_mm, s_onT = sem("onT_transposed"), sem("onT_ready")
        s_of_mm = sem("attn_out_done")
        s_x1b = sem("x1_plus_bias")
        s_r2, s_st2, s_ln2 = sem("residual2"), sem("stats2"), sem("ln2_steps")
        s_lnA2 = sem("ln2_act")
        s_x2 = sem("x2_ready")
        s_shift1, s_shift2 = sem("ln1_shift"), sem("ln2_shift")
        s_x2_st = sem("x2_stored")

        NP_, NV_ = len(POOL_STATES), len(DVE_STATES)
        consts = [
            (w_in, "w_in"), (w_x, "w_x"), (w_dt, "w_dt"), (w_out, "w_out"), (w_q, "w_q"), (w_k, "w_k"),
            (w_v, "w_v"), (w_o, "w_o"), (b_in, "b_in"), (conv_w, "conv_w"), (conv_b, "conv_b"),
            (b_dt, "b_dt"), (a_neg, "a_log"), (b_q, "b_q"), (b_k, "b_k"), (ident, "ident"),
        ]
        N_CONST = len(consts) + 3 + 1
        STACK_DMAS = 9

        def state_done(eng, n, batch, sem_p, sem_v):
            if n in POOL_STATES:
                if batch:
                    eng.wait_ge(sem_p, batch.value(NP_, POOL_STATES.index(n) + 1))
            else:
                if batch:
                    eng.wait_ge(sem_v, batch.value(NV_, DVE_STATES.index(n) + 1))

        def over_channels(row):
            return row.unsqueeze(1).to_broadcast([P, ND, L])

        block = ctx.enter_context(nc.Block())

        @block.sync
        def _(sp):
            counts = [sp.alloc_register(f"count_{i}") for i in range(6)]
            for tile, name in consts:
                sp.dma_start(tile[:], io[name]).then_inc(s_const, 16)
            for tile, name in ((b_out, "b_out"), (b_v, "b_v"), (b_o, "b_o")):
                sp.dma_start(tile[:], io[name].partition_broadcast(P)).then_inc(s_const, 16)
            sp.dma_start(h[:].rearrange("p a d t -> p (a d t)"), io["sel"]).then_inc(s_const, 16)
            sp.wait_ge(s_const_v, 10)

            def load_x(b):
                src = of_batch(sp, io["xT"], b)
                wait_all(sp, counts, (s_in_mm, 2 * ND, b.back(1), 2 * ND))
                sp.dma_start(xT[:], src).then_inc(s_xT, 16)

            def load_x_tok(b):
                src = of_batch(sp, io["x_tok"], b)
                wait_all(sp, counts, (s_r1, 1, b.back(1), 1))
                sp.dma_start(x_tok[:], src).then_inc(s_xtok, 16)

            def load_ctx(b):
                src = of_batch(sp, io["ctxT"], b)
                wait_all(sp, counts, (s_k_mm, KD, b.back(1), KD), (s_v_mm, TT, b.back(1), TT))
                sp.dma_start(ctxT[:], src).then_inc(s_ctxT, 16)

            def store_parts(dram, hi, lo, done):
                def piece(b):
                    wait_all(sp, counts, (hi, KD, b, KD), (lo, KD, b, KD),
                             *[(s, STACK_DMAS * 16, b.back(2), STACK_DMAS * 16) for s in s_stack])
                    dst = dram[b.par].rearrange("c (m p) t -> p c m t", p=P)
                    sp.dma_start(dst, parts[:].bitcast(F32)).then_inc(done, 16)
                return piece

            def load_stack(gr):
                def piece(b):
                    heads = slice(HG * gr, HG * gr + HG)
                    wait_all(sp, counts, (s_q_dram, 16, b, 16), (s_k_dram, 16, b, 16),
                             (s_st_mm, H, b.back(1), HG * gr + HG))
                    for row in range(4):
                        rows = slice(DK * row, DK * row + DK)
                        for stack, dram, part in ((q_st, q_dram, row // 2), (k_st, k_dram, row % 2)):
                            src = dram[b.par, part].rearrange("(h i) t -> i h t", i=DK)[:, heads, :]
                            sp.dma_start(stack[rows, heads, :].bitcast(F32), src).then_inc(s_stack[gr], 16)
                    sp.dma_start(q_st[4 * DK:4 * DK + 2, heads, :].bitcast(F32),
                                 k_st[4 * DK + 2:4 * DK + 4, heads, :].bitcast(F32)).then_inc(s_stack[gr], 16)
                return piece

            def store_x2(b):
                rows = x2_dram.rearrange("(a e n r) d -> n e r a d", a=TT, e=P // EC, r=EC)
                rows = rows[bass.ds(number(sp, b), 1)].rearrange("n e r a d -> (n e) r a d")
                wait_all(sp, counts, (s_x2, TT, b, TT))
                for q in range(P // EC):
                    sp.dma_start(rows[q], r2[EC * q:EC * (q + 1)]).then_inc(s_x2_st, 16)

            run_steps(sp, [
                (0, load_x),
                (34, load_x_tok),
                (38, load_ctx),
                (O_K + 2, store_parts(k_dram, s_k_hi, s_k_lo, s_k_dram)),
                (O_Q + 2, store_parts(q_dram, s_q_hi, s_q_lo, s_q_dram)),
                *[(O_LD + HG * gr, load_stack(gr)) for gr in range(NG)],
                (O_N2, store_x2),
            ], B, STEPS_DEEP)
            sp.wait_ge(s_x2_st, 16 * B * (P // EC))
            sp.wait_ge(s_q_dram, 16 * B)
            sp.wait_ge(s_k_dram, 16 * B)
            sp.wait_ge(s_m_dram, 16 * B * NG)

        @block.gpsimd
        def _(pool):
            pool.wait_ge(s_const, 16 * N_CONST)

            def dBu_piece(n):
                def piece(b):
                    pool.wait_ge(s_spv, b.value(4, 4))
                    pool.wait_ge(s_bc_sb, b.value(NS, n + 1))
                    if n >= 4:
                        pool.wait_ge(s_scan, b.value(NS, n - 3))
                    else:
                        if b.back(1):
                            pool.wait_ge(s_scan, b.back(1).value(NS, NS + n - 3))
                    pool.tensor_tensor(dBu[:, n % 4], w[:, b.par], over_channels(bc_sb[:, n % 4, 0, :]),
                                       ALU.mult).then_inc(s_dBu_p, 1)
                return piece

            def hC_piece(n):
                def piece(b):
                    pool.wait_ge(s_scan, b.value(NS, n + 1))
                    pool.tensor_tensor(h[:, n % 4], h[:, n % 4], over_channels(bc_sb[:, n % 4, 1, :]),
                                       ALU.mult).then_inc(s_hC_p, 1)
                return piece

            def x_bias(b):
                pool.wait_ge(s_xtok, b.value(16, 16))
                pool.tensor_tensor(x_tok[:], x_tok[:], b_out[:].unsqueeze(1).to_broadcast([P, TT, D]),
                                   ALU.add).then_inc(s_xb, 1)

            def x1_bias(b):
                pool.wait_ge(s_x1, b.value(TT, TT))
                if b.back(1):
                    pool.wait_ge(s_r2, b.back(1).value(1, 1))
                pool.tensor_tensor(x1b[:], x1[:, b.par], b_o[:].unsqueeze(1).to_broadcast([P, TT, D]),
                                   ALU.add).then_inc(s_x1b, 1)

            run_steps(pool, [
                *[(O_SCAN + n + 1, hC_piece(n)) for n in POOL_STATES],
                *[(O_SCAN + n - 2, dBu_piece(n)) for n in POOL_STATES],
                (36, x_bias),
                (O_X1B, x1_bias),
            ], B, STEPS_DEEP)

        @block.scalar
        def _(act):
            act.wait_ge(s_const, 16 * N_CONST)
            nc.scalar.activation(a_neg[:], a_neg[:], ACT.Exp).then_inc(s_const_a, 1)
            nc.scalar.activation(sel[:].rearrange("p a m -> p (a m)"), h[:].rearrange("p a d t -> p (a d t)"),
                                 ACT.Copy).then_inc(s_const_a, 1)
            act.wait_ge(s_const_v, 9)

            def in_evac(m):
                def piece(b):
                    act.wait_ge(s_in_mm, b.value(2 * ND, m // 2 * 2 + 2))
                    if m < ND:
                        if b.back(1):
                            act.wait_ge(s_spv, b.back(1).value(4, 3))
                        dst = xc[:, m, TAPS - 1:]
                    else:
                        if b.back(2):
                            act.wait_ge(s_g, b.back(2).value(1, 1))
                        dst = gate[:, b.par, m - ND]
                    nc.scalar.activation(dst, a_ps[:, m % 2, :], ACT.Identity,
                                         bias=b_in[:, m:m + 1]).then_inc(s_in_ev, 1)
                return piece

            def silu(b):
                act.wait_ge(s_in_ev, b.value(2 * ND, 2 * ND))
                nc.scalar.activation(gate[:, b.par], gate[:, b.par], ACT.Silu).then_inc(s_silu, 1)
                act.wait_ge(s_conv, b.value(ND, ND))
                nc.scalar.activation(u[:], u[:], ACT.Silu).then_inc(s_silu, 1)

            def xp_evac(b):
                act.wait_ge(s_xp_mm, b.value(1, 1))
                if b.back(1):
                    act.wait_ge(s_bcs, b.back(1).value(2, 2))
                if b.back(1):
                    act.wait_ge(s_dt_mm, b.back(1).value(ND, ND))
                nc.scalar.activation(xp[:], a_ps[0:RANK + 2 * NS, 0, :], ACT.Copy).then_inc(s_xp, 1)

            def z_evac(d):
                def piece(b):
                    act.wait_ge(s_dt_mm, b.value(ND, d // 2 * 2 + 2))
                    if b.back(1):
                        act.wait_ge(s_spv, b.back(1).value(4, 2))
                    nc.scalar.activation(z[:, d], a_ps[:, d % 2, :], ACT.Identity,
                                         bias=b_dt[:, d:d + 1]).then_inc(s_z, 1)
                return piece

            def softplus_exp(b):
                act.wait_ge(s_z, b.value(ND, ND))
                if b.back(1):
                    act.wait_ge(s_spv, b.back(1).value(4, 3))
                nc.scalar.activation(e, z[:], ACT.Abs).then_inc(s_sp, 1)
                act.wait_ge(s_sp, b.value(4, 1))
                nc.scalar.activation(e, e, ACT.Exp, scale=-1.0).then_inc(s_sp, 1)
                act.wait_ge(s_sp, b.value(4, 2))
                if b.back(2):
                    act.wait_ge(s_out_mm, b.back(2).value(TT, TT))
                nc.scalar.activation(e1[:], e, ACT.Identity, bias=one[:, 0:1]).then_inc(s_sp, 1)

            def softplus_ln(b):
                act.wait_ge(s_spv, b.value(4, 1))
                act.wait_ge(s_sp, b.value(4, 3))
                nc.scalar.activation(e1[:], e1[:], ACT.Ln).then_inc(s_sp, 1)

            def norm_ln(i, s_steps, s_act, s_x):
                def piece(b):
                    act.wait_ge(s_steps, b.value(5, 5))
                    if b.back(1):
                        act.wait_ge(s_x, b.back(1).value(TT, TT))
                    nc.scalar.activation(rstd[:, i], ln_tmp[:, i, 4], ACT.Ln, bias=eps[:, 0:1],
                                         scale=1.0 / D).then_inc(s_act, 1)
                return piece

            def norm_exp(i, s_act):
                def piece(b):
                    act.wait_ge(s_act, b.value(2, 1))
                    nc.scalar.activation(rstd[:, i], rstd[:, i], ACT.Exp, scale=-0.5).then_inc(s_act, 1)
                return piece

            def decay(n):
                def piece(b):
                    act.wait_ge(s_spv, b.value(4, 3))
                    if n >= 2:
                        act.wait_ge(s_scan, b.value(NS, n - 1))
                    else:
                        if b.back(1):
                            act.wait_ge(s_scan, b.back(1).value(NS, NS + n - 1))
                    for d in range(ND):
                        last = nc.scalar.activation(
                            dA[:, n % 2, d, :, 1:],
                            delta[:, b.par, d].rearrange("p (c t) -> p c t", t=CH)[:, :, 1:],
                            ACT.Exp, scale=a_neg[:, d, n:n + 1])
                    last.then_inc(s_dA, 1)
                return piece

            def bc_evac(n):
                def piece(b):
                    act.wait_ge(s_bc_mm, b.value(NS, n + 1))
                    state_done(act, (n - 4) % NS, b if n >= 4 else b.back(1), s_hC_p, s_hC_v)
                    nc.scalar.activation(bc_sb[:, n % 4], bc_ps[:], ACT.Copy).then_inc(s_bc_sb, 1)
                return piece

            def x1T_evac(b):
                act.wait_ge(s_x1T_mm, b.value(1, 1))
                if b.back(3):
                    act.wait_ge(s_of_mm, b.back(3).value(TT, TT))
                nc.scalar.activation(x1T[:], a_ps[:], ACT.Copy).then_inc(s_x1T, 1)

            def high(bias, s_mm, s_hi, s_dram, steps_back):
                def piece_for(m):
                    def piece(b):
                        act.wait_ge(s_mm, b.value(KD, KD))
                        if b.back(steps_back):
                            act.wait_ge(s_dram, b.back(steps_back).value(16, 16))
                        nc.scalar.activation(parts[:, 0, m], a_ps[:, m, :], ACT.Identity,
                                             bias=bias[:, m:m + 1]).then_inc(s_hi, 1)
                    return piece
                return piece_for

            k_high = high(b_k, s_k_mm, s_k_hi, s_q_dram, 1)
            q_high = high(b_q, s_q_mm, s_q_hi, s_k_dram, 0)

            def softmax_exp(hd):
                def piece(b):
                    act.wait_ge(s_st_mm, b.value(H, hd + 1))
                    if hd >= 2:
                        act.wait_ge(s_pv, b.value(H, hd - 1))
                    else:
                        if b.back(1):
                            act.wait_ge(s_pv, b.back(1).value(H, H + hd - 1))
                    nc.scalar.activation(probs[:, hd % 2], st_ps[:], ACT.Exp,
                                         scale=float(DK) ** -0.5).then_inc(s_exp, 1)
                return piece

            def oT_evac(gr):
                def piece(b):
                    act.wait_ge(s_pv, b.value(H, HG * gr + HG))
                    before = b if gr >= 2 else b.back(1)
                    if before:
                        act.wait_ge(s_on_mm, before.value(NG, gr - 1 if gr >= 2 else NG + gr - 1))
                    nc.scalar.activation(oT[:, gr % 2], pv_ps[:], ACT.Copy).then_inc(s_oT, 1)
                return piece

            def onT_evac(b):
                act.wait_ge(s_onT_mm, b.value(1, 1))
                act.wait_ge(s_q_mm, b.ahead(2).value(KD, KD))
                nc.scalar.activation(onT[:], f_ps[:], ACT.Copy).then_inc(s_onT, 1)

            def max_store(gr):
                def piece(b):
                    act.wait_ge(s_m_lo, b.value(NG, gr + 1))
                    if b.back(1):
                        act.wait_ge(s_m_row, b.back(1).value(NG * 16, 16 * gr + 16))
                    act.dma_start(m_dram[gr].rearrange("c (r t) -> r c t", t=P),
                                  m_rows[:, gr % 2].bitcast(F32)).then_inc(s_m_dram, 16)
                return piece

            def max_load(gr):
                def piece(b):
                    act.wait_ge(s_m_dram, b.value(NG * 16, 16 * gr + 16))
                    act.wait_ge(s_s_mm, b.value(H, HG * gr + HG))
                    dst = q_st[4 * DK:4 * DK + 2, HG * gr:HG * gr + HG, :].rearrange("p h t -> p (h t)")
                    act.dma_start(dst.bitcast(F32), m_dram[gr]).then_inc(s_m_row, 16)
                return piece

            run_steps(act, [
                *[(O_IN + m // 2 + 1, in_evac(m)) for m in range(2 * ND)],
                (O_XP + 1, xp_evac),
                *[(O_DT + d // 2 + 1, z_evac(d)) for d in range(ND)],
                (O_X1T + 1, x1T_evac),
                (O_ONT + 1, onT_evac),
                *[(O_MT + HG * gr + 1, max_store(gr)) for gr in range(NG)],
                *[(O_MT + HG * gr + 2, max_load(gr)) for gr in range(NG)],
                *[(O_K + 1, k_high(m)) for m in range(KD)],
                *[(O_Q + 1, q_high(m)) for m in range(KD)],
                *[(O_SCAN + n - 2, bc_evac(n)) for n in range(NS)],
                *[(O_E + hd, softmax_exp(hd)) for hd in range(H)],
                *[(O_SCAN + n - 1, decay(n)) for n in range(NS)],
                *[(O_E + HG * gr + HG, oT_evac(gr)) for gr in range(NG)],
                (O_SILU, silu),
                (O_SP, softplus_exp),
                (O_LN, softplus_ln),
                (O_LN + 32, norm_ln(0, s_ln1, s_lnA1, s_x1)),
                (O_LN2, norm_ln(1, s_ln2, s_lnA2, s_x2)),
                (O_LN + 32, norm_exp(0, s_lnA1)),
                (O_LN2, norm_exp(1, s_lnA2)),
            ], B, STEPS_DEEP)

        @block.vector
        def _(dve):
            nc.vector.memset(one[:], 1.0).then_inc(s_const_v, 1)
            nc.vector.memset(eps[:], EPS).then_inc(s_const_v, 1)
            nc.vector.memset(xc[:, :, 0:TAPS - 1], 0.0).then_inc(s_const_v, 1)
            nc.vector.memset(dA[:], 0.0).then_inc(s_const_v, 1)
            nc.vector.memset(bcs[:].bitcast(F32), 0.0).then_inc(s_const_v, 1)
            nc.vector.memset(v[:], 1.0).then_inc(s_const_v, 1)
            nc.vector.memset(k_st[4 * DK:SK].bitcast(F32), 0.0).then_inc(s_const_v, 1)
            nc.vector.memset(q_st[4 * DK:SK].bitcast(F32), 0.0).then_inc(s_const_v, 1)
            dve.wait_ge(s_const_a, 1)
            nc.vector.tensor_scalar(a_neg[:], a_neg[:], -1.0, None, ALU.mult).then_inc(s_const_v, 1)
            dve.wait_ge(s_const_v, 7)
            nc.vector.memset(k_st[4 * DK:4 * DK + 2].bitcast(F32), 1.0).then_inc(s_const_v, 1)
            dve.wait_ge(s_const_a, 2)
            dve.wait_ge(s_const, 16 * N_CONST)

            def conv(d):
                def piece(b):
                    dve.wait_ge(s_in_ev, b.value(2 * ND, d + 1))
                    if b.back(1):
                        dve.wait_ge(s_spv, b.back(1).value(4, 4))
                    if b.back(1):
                        dve.wait_ge(s_xp_mm, b.back(1).value(1, 1))
                    nc.vector.tensor_scalar(u[:, d], xc[:, d, 0:L], conv_w[:, d, 0:1], conv_b[:, d:d + 1],
                                            ALU.mult, ALU.add).then_inc(s_conv1, 1)
                    dve.wait_ge(s_conv1, b.value(2 * ND, 2 * d + 1))
                    nc.vector.scalar_tensor_tensor(out=u[:, d], in0=xc[:, d, 1:L + 1], scalar=conv_w[:, d, 1:2],
                                                   in1=u[:, d], op0=ALU.mult, op1=ALU.add).then_inc(s_conv1, 1)
                    dve.wait_ge(s_conv1, b.value(2 * ND, 2 * d + 2))
                    nc.vector.scalar_tensor_tensor(out=u[:, d], in0=xc[:, d, 2:L + 2], scalar=conv_w[:, d, 2:3],
                                                   in1=u[:, d], op0=ALU.mult, op1=ALU.add).then_inc(s_conv, 1)
                return piece

            def bc_split(b):
                dve.wait_ge(s_xp, b.value(1, 1))
                if b.back(2):
                    dve.wait_ge(s_bc_mm, b.back(2).value(NS, NS))
                bc = xp[RANK:RANK + 2 * NS]
                nc.vector.tensor_copy(bcs[0:2 * NS, b.par], bc).then_inc(s_bcs, 1)
                dve.wait_ge(s_bcs, b.value(2, 1))
                nc.vector.tensor_tensor(bcs[2 * NS:4 * NS, b.par], bc, bcs[0:2 * NS, b.par].bitcast(F32),
                                        ALU.subtract).then_inc(s_bcs, 1)

            def softplus_rounding(b):
                dve.wait_ge(s_sp, b.value(4, 3))
                nc.vector.scalar_tensor_tensor(out=e, in0=e1[:], scalar=-1.0, in1=e,
                                               op0=ALU.add, op1=ALU.subtract).then_inc(s_spv, 1)
                dve.wait_ge(s_spv, b.value(4, 1))
                nc.vector.scalar_tensor_tensor(out=e, in0=z[:], scalar=0.0, in1=e,
                                               op0=ALU.max, op1=ALU.subtract).then_inc(s_spv, 1)

            def softplus_sum(b):
                dve.wait_ge(s_sp, b.value(4, 4))
                dve.wait_ge(s_spv, b.value(4, 2))
                if b.back(2):
                    dve.wait_ge(s_dA, b.back(2).value(NS, NS))
                nc.vector.tensor_tensor(delta[:, b.par], e, e1[:], ALU.add).then_inc(s_spv, 1)
                dve.wait_ge(s_spv, b.value(4, 3))
                dve.wait_ge(s_silu, b.value(2, 2))
                nc.vector.tensor_tensor(w[:, b.par], delta[:, b.par], u[:], ALU.mult).then_inc(s_spv, 1)

            def dBu_piece(n):
                def piece(b):
                    dve.wait_ge(s_bc_sb, b.value(NS, n + 1))
                    dve.wait_ge(s_spv, b.value(4, 4))
                    nc.vector.tensor_tensor(dBu[:, n % 4], w[:, b.par], over_channels(bc_sb[:, n % 4, 0, :]),
                                            ALU.mult).then_inc(s_dBu_v, 1)
                return piece

            def scan(n):
                def piece(b):
                    dve.wait_ge(s_dA, b.value(NS, n + 1))
                    state_done(dve, n, b, s_dBu_p, s_dBu_v)
                    before, b_before = (n - 4) % NS, b if n >= 4 else b.back(1)
                    if before in SUMMED:
                        if b_before:
                            dve.wait_ge(s_sum, b_before.value(len(SUMMED), SUMMED.index(before) + 1))
                    else:
                        if b_before:
                            dve.wait_ge(s_pair, b_before.value(len(PAIRED), PAIRED.index(before + 1) + 1))
                    nc.vector.tensor_tensor_scan(
                        h[:, n % 4].rearrange("p d t -> p (d t)"),
                        dA[:, n % 2].rearrange("p d c t -> p (d c t)"),
                        dBu[:, n % 4].rearrange("p d t -> p (d t)"), 0.0, ALU.mult, ALU.add).then_inc(s_scan, 1)
                return piece

            def hC_piece(n):
                def piece(b):
                    dve.wait_ge(s_scan, b.value(NS, n + 1))
                    nc.vector.tensor_tensor(h[:, n % 4], h[:, n % 4], over_channels(bc_sb[:, n % 4, 1, :]),
                                            ALU.mult).then_inc(s_hC_v, 1)
                return piece

            def pair_add(n):
                def piece(b):
                    state_done(dve, n - 1, b, s_hC_p, s_hC_v)
                    state_done(dve, n, b, s_hC_p, s_hC_v)
                    nc.vector.tensor_tensor(h[:, n % 4], h[:, n % 4], h[:, (n - 1) % 4], ALU.add).then_inc(s_pair, 1)
                return piece

            def gating(b):
                dve.wait_ge(s_sum, b.value(len(SUMMED), len(SUMMED)))
                dve.wait_ge(s_silu, b.value(2, 1))
                dve.wait_ge(s_spv, b.ahead(1).value(4, 3))
                nc.vector.tensor_tensor(g[:], y_ps[:], gate[:, b.par], ALU.mult).then_inc(s_g, 1)

            def residual(i, r, s_mm, s_add, src_ps, add, s_r, s_st, s_free, free_per):
                def piece(b):
                    dve.wait_ge(s_mm, b.value(TT, TT))
                    dve.wait_ge(s_add, b.value(1, 1))
                    if b.back(1):
                        dve.wait_ge(s_free, b.back(1).value(free_per, free_per))
                    nc.vector.tensor_tensor(r[:], src_ps[:], add[:], ALU.add).then_inc(s_r, 1)
                    dve.wait_ge(s_r, b.value(1, 1))
                    for tt in range(TT):
                        nc.vector.bn_stats(st[:, i, tt], r[:, tt]).then_inc(s_st, 1)
                return piece

            def moments(i, s_st, s_steps, s_act):
                def piece(b):
                    dve.wait_ge(s_st, b.value(TT, TT))
                    if b.back(1):
                        dve.wait_ge(s_act, b.back(1).value(2, 2))
                    t = ln_tmp[:, i]
                    nc.vector.tensor_tensor(t[:, 0], st[:, i, :, 1], st[:, i, :, 4], ALU.subtract).then_inc(s_steps, 1)
                    nc.vector.tensor_tensor(t[:, 1], st[:, i, :, 2], st[:, i, :, 5], ALU.add).then_inc(s_steps, 1)
                    nc.vector.tensor_tensor(t[:, 2], st[:, i, :, 1], st[:, i, :, 4], ALU.add).then_inc(s_steps, 1)
                    dve.wait_ge(s_steps, b.value(5, 1))
                    nc.vector.scalar_tensor_tensor(out=t[:, 3], in0=t[:, 0], scalar=float(D) / 4, in1=t[:, 0],
                                                   op0=ALU.mult, op1=ALU.mult).then_inc(s_steps, 1)
                    dve.wait_ge(s_steps, b.value(5, 4))
                    nc.vector.tensor_tensor(t[:, 4], t[:, 1], t[:, 3], ALU.add).then_inc(s_steps, 1)
                return piece

            def normalise(i, r, dst, s_act, s_steps, s_shift, s_x, s_free, free_per, free_back):
                def piece(b):
                    dve.wait_ge(s_act, b.value(2, 2))
                    dve.wait_ge(s_steps, b.value(5, 5))
                    nc.vector.scalar_tensor_tensor(out=shift[:, i], in0=ln_tmp[:, i, 2], scalar=-0.5,
                                                   in1=rstd[:, i], op0=ALU.mult, op1=ALU.mult).then_inc(s_shift, 1)
                    dve.wait_ge(s_shift, b.value(1, 1))
                    if s_free is not None:
                        if b.back(free_back):
                            dve.wait_ge(s_free, b.back(free_back).value(free_per, free_per))
                    for tt in range(TT):
                        nc.vector.tensor_scalar(dst(b)[:, tt], r[:, tt], rstd[:, i, tt:tt + 1],
                                                shift[:, i, tt:tt + 1], ALU.mult, ALU.add).then_inc(s_x, 1)
                return piece

            def low(bias, s_hi, s_lo):
                def piece_for(m):
                    def piece(b):
                        dve.wait_ge(s_hi, b.value(KD, KD))
                        nc.vector.scalar_tensor_tensor(out=parts[:, 1, m], in0=a_ps[:, m, :],
                                                       scalar=bias[:, m:m + 1], in1=parts[:, 0, m].bitcast(F32),
                                                       op0=ALU.add, op1=ALU.subtract).then_inc(s_lo, 1)
                    return piece
                return piece_for

            k_low, q_low = low(b_k, s_k_hi, s_k_lo), low(b_q, s_q_hi, s_q_lo)

            def v_evac(b):
                dve.wait_ge(s_v_mm, b.value(TT, TT))
                if b.back(2):
                    dve.wait_ge(s_pv, b.back(2).value(H, H))
                nc.vector.tensor_tensor(v[:, b.par, :, :, 0:DK],
                                        f_ps[:].rearrange("p a (h i) -> p a h i", i=DK),
                                        b_v[:].rearrange("p (h i) -> p h i", i=DK).unsqueeze(1)
                                        .to_broadcast([P, TT, H, DK]), ALU.add).then_inc(s_v, 1)

            def row_max(hd):
                def piece(b):
                    dve.wait_ge(s_s_mm, b.value(H, hd + 1))
                    if b.back(1):
                        dve.wait_ge(s_mT_mm, b.back(1).value(NG, hd // HG + 1))
                    nc.vector.tensor_reduce(mx[:, hd], s_ps[:], AX.X, ALU.max).then_inc(s_max, 1)
                return piece

            def max_parts(gr):
                def piece(b):
                    dve.wait_ge(s_mT_mm, b.value(NG, gr + 1))
                    if gr >= 2:
                        dve.wait_ge(s_m_dram, b.value(NG * 16, 16 * (gr - 1)))
                    else:
                        if b.back(1):
                            dve.wait_ge(s_m_dram, b.back(1).value(NG * 16, 16 * (NG + gr - 1)))
                    src = s_ps[0:HG * TT, 0, 0:P]
                    nc.vector.tensor_scalar(m_rows[:, gr % 2, 0], src, -1.0, None, ALU.mult).then_inc(s_m_hi, 1)
                    dve.wait_ge(s_m_hi, b.value(NG, gr + 1))
                    nc.vector.scalar_tensor_tensor(out=m_rows[:, gr % 2, 1], in0=src, scalar=-1.0,
                                                   in1=m_rows[:, gr % 2, 0].bitcast(F32), op0=ALU.mult,
                                                   op1=ALU.subtract).then_inc(s_m_lo, 1)
                return piece

            def head_norm(gr):
                def piece(b):
                    dve.wait_ge(s_on_mm, b.value(NG, gr + 1))
                    src = f_ps[:, 0, :].rearrange("p (a h i) -> p a h i", a=TT, h=HG)
                    if gr:
                        dve.wait_ge(s_on, b.value(NG, gr))
                    else:
                        if b.back(1):
                            dve.wait_ge(s_on, b.back(1).value(NG, NG))
                    nc.vector.reciprocal(rsum[:], src[:, :, :, DK]).then_inc(s_rsum, 1)
                    dve.wait_ge(s_rsum, b.value(NG, gr + 1))
                    if b.back(1):
                        dve.wait_ge(s_onT_mm, b.back(1).value(1, 1))
                    dst = on[:, :, HG * DK * gr:HG * DK * (gr + 1)].rearrange("p a (h i) -> p a h i", i=DK)
                    nc.vector.tensor_tensor(dst, src[:, :, :, 0:DK],
                                            rsum[:].unsqueeze(3).to_broadcast([P, TT, HG, DK]),
                                            ALU.mult).then_inc(s_on, 1)
                return piece

            run_steps(dve, [
                (O_OUT + 1, residual(0, r1, s_out_mm, s_xb, a_ps, x_tok, s_r1, s_st1, s_x1, TT)),
                (O_OF + 1, residual(1, r2, s_of_mm, s_x1b, f_ps, x1b, s_r2, s_st2, s_x2_st, 16 * P // EC)),
                (O_G, gating),
                *[(O_SCAN + n + 1, hC_piece(n)) for n in DVE_STATES],
                *[(O_S + hd + 1, row_max(hd)) for hd in range(H)],
                *[(O_SCAN + n + 2, pair_add(n)) for n in PAIRED],
                *[(O_MT + HG * gr, max_parts(gr)) for gr in range(NG)],
                *[(O_SCAN + n, scan(n)) for n in range(NS)],
                *[(O_SCAN + n - 1, dBu_piece(n)) for n in DVE_STATES],
                *[(O_CONV + d // 2, conv(d)) for d in range(ND)],
                (O_XP + 1, bc_split),
                (O_SP + 1, softplus_rounding),
                (O_W, softplus_sum),
                (O_OUT + 2, moments(0, s_st1, s_ln1, s_lnA1)),
                (O_N1, normalise(0, r1, lambda b: x1[:, b.par], s_lnA1, s_ln1, s_shift1, s_x1, s_x1b, 1, 2)),
                *[(O_K + 1, k_low(m)) for m in range(KD)],
                *[(O_Q + 1, q_low(m)) for m in range(KD)],
                (O_V + 1, v_evac),
                *[(O_ON + HG * gr + 1, head_norm(gr)) for gr in range(NG)],
                (O_OF + 2, moments(1, s_st2, s_ln2, s_lnA2)),
                (O_N2, normalise(1, r2, lambda b: r2[:], s_lnA2, s_ln2, s_shift2, s_x2, None, 0, 0)),
            ], B, STEPS_DEEP)

        @block.tensor
        def _(pe):
            pe.wait_ge(s_const, 16 * N_CONST)
            pe.wait_ge(s_const_a, 2)
            pe.wait_ge(s_const_v, 10)
            bank_a, bank_f, bank_s = Bank(), Bank(), Bank()

            def mm(out, lhsT, rhs, first, last):
                return nc.tensor.matmul(out, lhsT, rhs, start=first, stop=last)

            def in_proj(m):
                def piece(b):
                    pe.wait_ge(s_xT, b.value(16, 16))
                    if m % 2 == 0:
                        bank_a.wait_read(pe, b.j)
                    for k in range(KD):
                        i = mm(a_ps[:, m % 2, :], w_in[:, k, m * P:(m + 1) * P], xT[:, k], k == 0, k == KD - 1)
                    i.then_inc(s_in_mm, 1)
                    bank_a.read_by(s_in_ev, 2 * ND, b, m + 1)
                return piece

            def x_proj(b):
                pe.wait_ge(s_silu, b.value(2, 2))
                bank_a.wait_read(pe, b.j)
                for k in range(ND):
                    i = mm(a_ps[0:RANK + 2 * NS, 0, :], w_x[:, k], u[:, k], k == 0, k == ND - 1)
                i.then_inc(s_xp_mm, 1)
                bank_a.read_by(s_xp, 1, b, 1)

            def dt_proj(d):
                def piece(b):
                    pe.wait_ge(s_xp, b.value(1, 1))
                    if d % 2 == 0:
                        bank_a.wait_read(pe, b.j)
                    mm(a_ps[:, d % 2, :], w_dt[:, d * P:(d + 1) * P], xp[:], True, True).then_inc(s_dt_mm, 1)
                    bank_a.read_by(s_z, ND, b, d + 1)
                return piece

            def broadcast(n):
                def piece(b):
                    pe.wait_ge(s_bcs, b.value(2, 2))
                    before = b if n else b.back(1)
                    if before:
                        pe.wait_ge(s_bc_sb, before.value(NS, n or NS))
                    mm(bc_ps[:, 0, :], sel[:, n], bcs[:, b.par], True, True)
                    mm(bc_ps[:, 1, :], sel[:, NS + n], bcs[:, b.par], True, True).then_inc(s_bc_mm, 1)
                return piece

            def state_sum(n):
                def piece(b):
                    if n in PAIRED:
                        pe.wait_ge(s_pair, b.value(len(PAIRED), PAIRED.index(n) + 1))
                    else:
                        state_done(pe, n, b, s_hC_p, s_hC_v)
                    if n == SUMMED[0]:
                        if b.back(1):
                            pe.wait_ge(s_g, b.back(1).value(1, 1))
                    for c in range(2):
                        i = mm(y_ps[:, 2 * c:2 * c + 2].rearrange("p d t -> p (d t)"), ident[:],
                               h[:, n % 4, 2 * c:2 * c + 2].rearrange("p d t -> p (d t)"), n == SUMMED[0], n == NS - 1)
                    i.then_inc(s_sum, 1)
                return piece

            def out_proj(tt):
                def piece(b):
                    pe.wait_ge(s_g, b.value(1, 1))
                    if tt == 0:
                        bank_a.wait_read(pe, b.j)
                    for k in range(ND):
                        i = mm(a_ps[:, tt, :], g[:, k, tt * P:(tt + 1) * P], w_out[:, k], k == 0, k == ND - 1)
                    i.then_inc(s_out_mm, 1)
                    bank_a.read_by(s_r1, 1, b, 1)
                return piece

            def k_proj(m):
                def piece(b):
                    pe.wait_ge(s_ctxT, b.value(16, 16))
                    if m == 0:
                        bank_a.wait_read(pe, b.j)
                    for k in range(KD):
                        i = mm(a_ps[:, m, :], w_k[:, k, m * P:(m + 1) * P], ctxT[:, k], k == 0, k == KD - 1)
                    i.then_inc(s_k_mm, 1)
                    bank_a.read_by(s_k_lo, KD, b, m + 1)
                return piece

            def v_proj(tt):
                def piece(b):
                    pe.wait_ge(s_ctxT, b.value(16, 16))
                    if tt == 0:
                        bank_f.wait_read(pe, b.j)
                    for k in range(KD):
                        i = mm(f_ps[:, tt, :], ctxT[:, k, tt * P:(tt + 1) * P], w_v[:, k], k == 0, k == KD - 1)
                    i.then_inc(s_v_mm, 1)
                    bank_f.read_by(s_v, 1, b, 1)
                return piece

            def transpose(src, s_src, per, s_mm, s_read, bank, dst):
                def piece(b):
                    pe.wait_ge(s_src, b.value(per, per))
                    bank.wait_read(pe, b.j)
                    for k in range(KD):
                        for tt in range(TT):
                            i = nc.tensor.transpose(dst[:, k, tt * P:(tt + 1) * P],
                                                    src(b)[:, tt, k * P:(k + 1) * P], ident[:])
                    i.then_inc(s_mm, 1)
                    bank.read_by(s_read, 1, b, 1)
                return piece

            def q_proj(m):
                def piece(b):
                    pe.wait_ge(s_x1T, b.value(1, 1))
                    if m == 0:
                        bank_a.wait_read(pe, b.j)
                    for k in range(KD):
                        i = mm(a_ps[:, m, :], w_q[:, k, m * P:(m + 1) * P], x1T[:, k], k == 0, k == KD - 1)
                    i.then_inc(s_q_mm, 1)
                    bank_a.read_by(s_q_lo, KD, b, m + 1)
                return piece

            def scores(hd):
                def piece(b):
                    pe.wait_ge(s_stack[hd // HG], b.value(STACK_DMAS * 16, STACK_DMAS * 16))
                    bank_s.wait_read(pe, b.j)
                    for tt in range(TT):
                        i = mm(s_ps[:, tt], q_st[:, hd, tt * P:(tt + 1) * P], k_st[:, hd], True, True)
                    i.then_inc(s_s_mm, 1)
                    bank_s.read_by(s_max, H, b, hd + 1)
                return piece

            def max_transpose(gr):
                def piece(b):
                    pe.wait_ge(s_max, b.value(H, HG * gr + HG))
                    bank_s.wait_read(pe, b.j)
                    nc.tensor.transpose(s_ps[0:HG * TT, 0, 0:P],
                                        mx[:, HG * gr:HG * gr + HG].rearrange("p h a -> p (h a)"),
                                        ident[:]).then_inc(s_mT_mm, 1)
                    bank_s.read_by(s_m_lo, NG, b, gr + 1)
                return piece

            def scores_T(hd):
                def piece(b):
                    pe.wait_ge(s_m_row, b.value(NG * 16, 16 * (hd // HG) + 16))
                    before = b if hd else b.back(1)
                    if before:
                        pe.wait_ge(s_exp, before.value(H, hd or H))
                    for kt in range(TT):
                        i = mm(st_ps[:, kt], k_st[:, hd, kt * P:(kt + 1) * P], q_st[:, hd], True, True)
                    i.then_inc(s_st_mm, 1)
                return piece

            def pv(hd):
                def piece(b):
                    pe.wait_ge(s_exp, b.value(H, hd + 1))
                    pe.wait_ge(s_v, b.value(1, 1))
                    if hd % HG == 0:
                        gr = hd // HG
                        before = b if gr else b.back(1)
                        if before:
                            pe.wait_ge(s_oT, before.value(NG, gr or NG))
                    j = hd % HG
                    for kt in range(TT):
                        i = mm(pv_ps[2 * DK * j:2 * DK * (j + 1)], v[:, b.par, kt, hd], probs[:, hd % 2, kt],
                               kt == 0, kt == TT - 1)
                    i.then_inc(s_pv, 1)
                return piece

            def head_transpose(gr):
                def piece(b):
                    pe.wait_ge(s_oT, b.value(NG, gr + 1))
                    bank_f.wait_read(pe, b.j)
                    for tt in range(TT):
                        i = nc.tensor.transpose(f_ps[:, 0, tt * P:(tt + 1) * P], oT[:, gr % 2, tt * P:(tt + 1) * P],
                                                ident[:])
                    i.then_inc(s_on_mm, 1)
                    bank_f.read_by(s_on, NG, b, gr + 1)
                return piece

            def attn_out(tt):
                def piece(b):
                    pe.wait_ge(s_onT, b.value(1, 1))
                    if tt == 0:
                        bank_f.wait_read(pe, b.j)
                    for k in range(KD):
                        i = mm(f_ps[:, tt, :], onT[:, k, tt * P:(tt + 1) * P], w_o[:, k], k == 0, k == KD - 1)
                    i.then_inc(s_of_mm, 1)
                    bank_f.read_by(s_r2, 1, b, 1)
                return piece

            run_steps(pe, [
                *[(O_SCAN + n - 2, broadcast(n)) for n in range(NS)],
                *[(O_E + hd, scores_T(hd)) for hd in range(H)],
                *[(O_SCAN + n + 3, state_sum(n)) for n in SUMMED[1:]],
                *[(O_MT + HG * gr, max_transpose(gr)) for gr in range(NG)],
                *[(O_E + hd + 1, pv(hd)) for hd in range(H)],
                *[(O_IN + m // 2, in_proj(m)) for m in range(2 * ND)],
                (O_XP, x_proj),
                *[(O_DT + d // 2, dt_proj(d)) for d in range(ND)],
                *[(O_OUT, out_proj(tt)) for tt in range(TT)],
                *[(O_K, k_proj(m)) for m in range(KD)],
                *[(O_V, v_proj(tt)) for tt in range(TT)],
                (O_X1T, transpose(lambda b: x1[:, b.par], s_x1, TT, s_x1T_mm, s_x1T, bank_a, a_ps)),
                *[(O_Q, q_proj(m)) for m in range(KD)],
                *[(O_ON + HG * gr, head_transpose(gr)) for gr in range(NG)],
                (O_ONT, transpose(lambda b: on[:], s_on, NG, s_onT_mm, s_onT, bank_f, f_ps)),
                *[(O_OF, attn_out(tt)) for tt in range(TT)],
                *[(O_S + hd, scores(hd)) for hd in range(H)],
                (O_SCAN + SUMMED[0] + 3, state_sum(SUMMED[0])),
            ], B, STEPS_DEEP, (bank_a, bank_f, bank_s))


def experts(nc, io, x2_dram, out):
    with ExitStack() as ctx:
        def sb(name, shape, dt=F32):
            return ctx.enter_context(nc.sbuf_tensor(name, shape, dt))

        def sem(name):
            return ctx.enter_context(nc.semaphore(name))

        HALF = ET // 2
        ident = sb("ident_ffn", [P, P])
        eps = sb("eps_ffn", [P, 1])
        w1, w3 = sb("w1", [P, 2, KD, FF]), sb("w3", [P, 2, KD, FF])
        w2 = sb("w2", [P, 2, FT, D])
        x2 = sb("x2", [P, 2, EJ, D])
        x2T = sb("x2T", [P, KD, ET])
        hT = sb("hT", [P, FT, ET])
        silu = sb("silu", [P, 2, HALF])
        st = sb("st_ffn", [P, 2, EJ, 6])
        tmp = sb("ln_tmp_ffn", [P, 5, EJ])
        rstd, shift = sb("rstd_ffn", [P, EJ]), sb("shift_ffn", [P, EJ])

        def bank(name):
            return ctx.enter_context(nc.psum_tensor(name, [P, HALF], F32))

        t_ps, g_ps, u_ps, d_ps = ([bank(f"{n}{i}") for i in range(2)] for n in ("t_ps", "g_ps", "u_ps", "d_ps"))

        f_const, f_const_v = sem("ffn_const_loaded"), sem("ffn_const_set")
        f_x, f_w13, f_w2 = ([sem(f"{n}_loaded_{i}") for i in range(2)] for n in ("x2", "w13", "w2"))
        f_t_mm, f_t = sem("x2T_transposed"), sem("x2T_ready")
        f_g_mm, f_u_mm = sem("gate_done"), sem("up_done")
        f_silu, f_h = sem("silu_ready"), sem("h_ready")
        f_d_mm, f_r, f_st = sem("down_done"), sem("residual3"), sem("stats3")
        f_ln, f_act, f_shift, f_n = sem("ln3_steps"), sem("ln3_act"), sem("ln3_shift"), sem("normalised3")
        f_out = sem("out_stored")
        OUTS = P // EC

        block = ctx.enter_context(nc.Block())

        @block.sync
        def _(sp):
            counts = [sp.alloc_register(f"expert_count_{i}") for i in range(4)]
            sp.dma_start(ident[:], io["ident"]).then_inc(f_const, 16)
            sp.wait_ge(f_const_v, 3)

            def load(b):
                e_at = bass.ds(number(sp, b), 1)
                tokens = x2_dram.rearrange("(e j p) d -> e p j d", e=E, p=P)[e_at]
                wait_all(sp, counts, (f_out, 16 * OUTS, b.back(2), 16 * OUTS))
                sp.dma_start(x2[:, b.par], tokens.rearrange("a p j d -> (a p) j d")).then_inc(f_x[b.par], 16)
                wait_all(sp, counts, (f_d_mm, EJ, b.back(2), EJ))
                for tile, name in ((w1, "w1"), (w3, "w3")):
                    src = io[name].rearrange("e (k p) f -> e p k f", p=P)[e_at]
                    sp.dma_start(tile[:, b.par], src.rearrange("a p k f -> (a p) k f")).then_inc(f_w13[b.par], 16)
                full = (FT - 1) * P
                src = io["w2"][e_at, 0:full].rearrange("a (k p) d -> (a p) k d", p=P)
                sp.dma_start(w2[:, b.par, 0:FT - 1], src).then_inc(f_w2[b.par], 16)
                src = io["w2"][e_at, full:FF].rearrange("a p d -> (a p) d")
                sp.dma_start(w2[0:FL, b.par, FT - 1], src).then_inc(f_w2[b.par], 16)

            def store(b):
                rows = out.rearrange("(j q) (e r) d -> e q r j d", q=OUTS, r=EC)
                rows = rows[bass.ds(number(sp, b), 1)].rearrange("a q r j d -> (a q) r j d")
                wait_all(sp, counts, (f_n, EJ, b, EJ))
                for q in range(OUTS):
                    sp.dma_start(rows[q], x2[EC * q:EC * (q + 1), b.par]).then_inc(f_out, 16)

            run_steps(sp, [(SLOTS + 2, store), (0, load)], E, 1)
            sp.wait_ge(f_out, 16 * OUTS * E)

        @block.scalar
        def _(act):
            act.wait_ge(f_const_v, 3)

            def xT_evac(b):
                if b.back(1):
                    act.wait_ge(f_u_mm, b.back(1).value(2 * FT, 2 * FT))
                for i in range(2 * KD):
                    act.wait_ge(f_t_mm, b.value(2 * KD, i + 1))
                    nc.scalar.activation(x2T[:, i // 2, HALF * (i % 2):HALF * (i % 2 + 1)], t_ps[i % 2][:],
                                         ACT.Copy).then_inc(f_t, 1)

            def gates(b):
                for i in range(2 * FT):
                    m = P if i // 2 < FT - 1 else FL
                    act.wait_ge(f_g_mm, b.value(2 * FT, i + 1))
                    if i >= 2:
                        act.wait_ge(f_h, b.value(2 * FT, i - 1))
                    else:
                        if b.back(1):
                            act.wait_ge(f_h, b.back(1).value(2 * FT, 2 * FT + i - 1))
                    nc.scalar.activation(silu[0:m, i % 2], g_ps[i % 2][0:m], ACT.Silu).then_inc(f_silu, 1)

            def norm(b):
                act.wait_ge(f_ln, b.value(5, 5))
                if b.back(1):
                    act.wait_ge(f_n, b.back(1).value(EJ, EJ))
                nc.scalar.activation(rstd[:], tmp[:, 4], ACT.Ln, bias=eps[:, 0:1], scale=1.0 / D).then_inc(f_act, 1)
                act.wait_ge(f_act, b.value(2, 1))
                nc.scalar.activation(rstd[:], rstd[:], ACT.Exp, scale=-0.5).then_inc(f_act, 1)

            run_steps(act, [(0, xT_evac), (1, gates), (SLOTS + 2, norm)], E, 1)

        @block.vector
        def _(dve):
            nc.vector.memset(eps[:], EPS).then_inc(f_const_v, 1)
            nc.vector.memset(w2[FL:P, :, FT - 1], 0.0).then_inc(f_const_v, 1)
            nc.vector.memset(hT[FL:P, FT - 1], 0.0).then_inc(f_const_v, 1)
            dve.wait_ge(f_const_v, 3)

            def products(b):
                if b.back(1):
                    dve.wait_ge(f_d_mm, b.back(1).value(EJ, EJ))
                for i in range(2 * FT):
                    m = P if i // 2 < FT - 1 else FL
                    dve.wait_ge(f_silu, b.value(2 * FT, i + 1))
                    dve.wait_ge(f_u_mm, b.value(2 * FT, i + 1))
                    nc.vector.tensor_tensor(hT[0:m, i // 2, HALF * (i % 2):HALF * (i % 2 + 1)], silu[0:m, i % 2],
                                            u_ps[i % 2][0:m], ALU.mult).then_inc(f_h, 1)

            def normalise(b):
                dve.wait_ge(f_act, b.value(2, 2))
                nc.vector.scalar_tensor_tensor(out=shift[:], in0=tmp[:, 2], scalar=-0.5, in1=rstd[:],
                                               op0=ALU.mult, op1=ALU.mult).then_inc(f_shift, 1)
                dve.wait_ge(f_shift, b.value(1, 1))
                for t in range(EJ):
                    nc.vector.tensor_scalar(x2[:, b.par, t], x2[:, b.par, t], rstd[:, t:t + 1], shift[:, t:t + 1],
                                            ALU.mult, ALU.add).then_inc(f_n, 1)

            def residuals(b):
                for t in range(EJ):
                    dve.wait_ge(f_d_mm, b.value(EJ, t + 1))
                    nc.vector.tensor_tensor(x2[:, b.par, t], d_ps[t % 2][:, 0:D], x2[:, b.par, t],
                                            ALU.add).then_inc(f_r, 1)
                    dve.wait_ge(f_r, b.value(EJ, t + 1))
                    nc.vector.bn_stats(st[:, b.par, t], x2[:, b.par, t]).then_inc(f_st, 1)

            def moments(b):
                dve.wait_ge(f_st, b.value(EJ, EJ))
                s = st[:, b.par]
                nc.vector.tensor_tensor(tmp[:, 0], s[:, :, 1], s[:, :, 4], ALU.subtract).then_inc(f_ln, 1)
                nc.vector.tensor_tensor(tmp[:, 1], s[:, :, 2], s[:, :, 5], ALU.add).then_inc(f_ln, 1)
                nc.vector.tensor_tensor(tmp[:, 2], s[:, :, 1], s[:, :, 4], ALU.add).then_inc(f_ln, 1)
                dve.wait_ge(f_ln, b.value(5, 1))
                nc.vector.scalar_tensor_tensor(out=tmp[:, 3], in0=tmp[:, 0], scalar=float(D) / 4, in1=tmp[:, 0],
                                               op0=ALU.mult, op1=ALU.mult).then_inc(f_ln, 1)
                dve.wait_ge(f_ln, b.value(5, 4))
                nc.vector.tensor_tensor(tmp[:, 4], tmp[:, 1], tmp[:, 3], ALU.add).then_inc(f_ln, 1)

            run_steps(dve, [(1, products), (SLOTS + 2, normalise), (3, residuals), (4, moments)], E, 1)

        @block.tensor
        def _(pe):
            pe.wait_ge(f_const, 16)
            pe.wait_ge(f_const_v, 3)

            def transposes(b):
                pe.wait_ge(f_x[b.par], b.same_parity(16))
                for i in range(2 * KD):
                    if i >= 2:
                        pe.wait_ge(f_t, b.value(2 * KD, i - 1))
                    else:
                        if b.back(1):
                            pe.wait_ge(f_t, b.back(1).value(2 * KD, 2 * KD + i - 1))
                    k = i // 2
                    for t in range(EJ // 2):
                        ins = nc.tensor.transpose(t_ps[i % 2][:, t * P:(t + 1) * P],
                                                  x2[:, b.par, EJ // 2 * (i % 2) + t, k * P:(k + 1) * P], ident[:])
                    ins.then_inc(f_t_mm, 1)

            def gate_up(b):
                pe.wait_ge(f_t, b.value(2 * KD, 2 * KD))
                pe.wait_ge(f_w13[b.par], b.same_parity(32))
                for i in range(2 * FT):
                    f0 = P * (i // 2)
                    m = min(P, FF - f0)
                    cols = slice(HALF * (i % 2), HALF * (i % 2 + 1))
                    for w_, ps, done, read in ((w1, g_ps, f_g_mm, f_silu), (w3, u_ps, f_u_mm, f_h)):
                        if i >= 2:
                            pe.wait_ge(read, b.value(2 * FT, i - 1))
                        else:
                            if b.back(1):
                                pe.wait_ge(read, b.back(1).value(2 * FT, 2 * FT + i - 1))
                        for k in range(KD):
                            ins = nc.tensor.matmul(ps[i % 2][0:m], w_[:, b.par, k, f0:f0 + m], x2T[:, k, cols],
                                                   start=(k == 0), stop=(k == KD - 1))
                        ins.then_inc(done, 1)

            def down(b):
                pe.wait_ge(f_w2[b.par], b.same_parity(32))
                pe.wait_ge(f_h, b.value(2 * FT, 2 * FT))
                for t in range(EJ):
                    if t >= 2:
                        pe.wait_ge(f_r, b.value(EJ, t - 1))
                    else:
                        if b.back(1):
                            pe.wait_ge(f_r, b.back(1).value(EJ, EJ + t - 1))
                    for k in range(FT):
                        ins = nc.tensor.matmul(d_ps[t % 2][:, 0:D], hT[:, k, t * P:(t + 1) * P], w2[:, b.par, k],
                                               start=(k == 0), stop=(k == FT - 1))
                    ins.then_inc(f_d_mm, 1)

            run_steps(pe, [(0, transposes), (1, gate_up), (3, down)], E, 1)


def decoder_layer(nc, io, out):
    x2_dram = nc.dram_tensor("x2_rows", (E * ET, D), F32, kind="Internal").ap()
    q_dram = nc.dram_tensor("q_parts_dram", (2, 2, D, L), F32, kind="Internal").ap()
    k_dram = nc.dram_tensor("k_parts_dram", (2, 2, D, L), F32, kind="Internal").ap()
    m_dram = nc.dram_tensor("max_rows_dram", (NG, 2, HG * L), F32, kind="Internal").ap()
    mixers(nc, io, x2_dram, q_dram, k_dram, m_dram)
    experts(nc, io, x2_dram, out)


def layouts(inputs):
    def columns(a, *shape):
        a = np.asarray(a)
        return a.reshape(-1, P, *a.shape[1:]).swapaxes(0, 1).reshape(P, -1, *shape)

    def tokens_last(a):
        return np.asarray(a).transpose(0, 2, 1).reshape(B, KD, P, L).transpose(0, 2, 1, 3)

    i = {k.removeprefix("L0_"): np.asarray(a) for k, a in inputs.items()}
    selector = np.zeros((P, 2 * NS, P), np.float32)
    for n in range(2 * NS):
        selector[[n, 2 * NS + n], n] = 1.0
    return {
        "xT": tokens_last(i["x"]),
        "x_tok": i["x"].reshape(B, TT, P, D).transpose(0, 2, 1, 3),
        "ctxT": tokens_last(i["ctx_1024"]),
        "w_in": columns(i["attn_W_in"].T, 2 * DI),
        "w_x": columns(i["attn_W_x"].T, RANK + 2 * NS),
        "w_dt": np.concatenate([i["attn_W_dt"].T, np.zeros((2 * NS, DI), np.float32)]),
        "w_out": columns(i["attn_W_out"].T, D),
        "w_q": columns(i["xattn_w_q"].T, D), "w_k": columns(i["xattn_w_k"].T, D),
        "w_v": columns(i["xattn_w_v"].T, D), "w_o": columns(i["xattn_w_o"].T, D),
        "b_in": columns(i["attn_b_in"]), "conv_w": columns(i["attn_conv_w"][:, 0], TAPS),
        "conv_b": columns(i["attn_conv_b"]), "b_dt": columns(i["attn_b_dt"]),
        "a_log": columns(i["attn_A_log"], NS),
        "b_q": columns(i["xattn_b_q"]), "b_k": columns(i["xattn_b_k"]),
        "b_out": i["attn_b_out"], "b_v": i["xattn_b_v"], "b_o": i["xattn_b_o"],
        "w1": i["ffn_w1"], "w3": i["ffn_w3"], "w2": i["ffn_w2"],
        "ident": np.eye(P, dtype=np.float32),
        "sel": selector.reshape(P, 2 * NS * P),
    }


def kernel(**inputs):
    import concourse.bacc as bacc
    from concourse.bass_utils import run_bass_kernel_spmd

    nc = bacc.Bacc("TRN2", target_bir_lowering=False, num_devices=1)
    arrays = {f"in_{k}": np.ascontiguousarray(a) for k, a in layouts(inputs).items()}
    io = {k.removeprefix("in_"): nc.dram_tensor(k, a.shape, mybir.dt.from_np(a.dtype), kind="ExternalInput").ap()
          for k, a in arrays.items()}
    out = nc.dram_tensor("out", (B, L, D), F32, kind="ExternalOutput").ap()
    decoder_layer(nc, io, out)
    result = run_bass_kernel_spmd(nc, [arrays], core_ids=[0])
    return result.results[0]["out"]
```
